# Optimizing a Trainium2 kernel written in Bass

```python
import numpy as np
import jax
import jax.numpy as jnp

def _softmax(x, axis=-1):
    return jax.nn.softmax(x, axis=axis)
def _gelu(x):
    return jax.nn.gelu(x, approximate=True)
def _silu(x):
    return jax.nn.silu(x)
def _sigmoid(x):
    return jax.nn.sigmoid(x)
def _layernorm(x, axis=-1, eps=1e-5):
    m = jnp.mean(x, axis=axis, keepdims=True)
    v = jnp.var(x, axis=axis, keepdims=True)
    return (x - m) / jnp.sqrt(v + eps)
def _scatter_add(tgt, idx, src, axis=0):
    return tgt.at[idx].add(src)
def _segment_sum(src, seg, n):
    return jax.ops.segment_sum(src, seg, n)

kernel_name = 'mk_conv_seq_d2_conv_nchw128_3a292f'

def setup_inputs(seed: int = 0):
    np.random.seed(seed)
    _w = jnp.asarray
    def _rec_inputs():
        import jax
        import jax.numpy as jnp
        _gk = jax.random.key(seed)
        x = -0.0003929 + 0.9999 * jax.random.normal(jax.random.fold_in(_gk, 1), (8, 128, 128, 128), jnp.float32)
        return x
    x = _rec_inputs()
    def _L0_conv_setup():
        import jax, jax.numpy as jnp
        import numpy as np
        BN_EPS = 1e-05
        EPS = 1e-06

        def _conv(x, w, pad, dil):
            return jax.lax.conv_general_dilated(x, w, window_strides=(1, 1), padding=[(pad, pad), (pad, pad)], rhs_dilation=(dil, dil), dimension_numbers=('NCHW', 'OIHW', 'NCHW'))

        def _bn_relu(x, s, b, m, v):
            inv = (s / jnp.sqrt(v + BN_EPS))[None, :, None, None]
            return jax.nn.relu((x - m[None, :, None, None]) * inv + b[None, :, None, None])

        def _l2n(x):
            return x / jnp.linalg.norm(x, axis=1, keepdims=True)

        def _forward(x, w1, w2, w3, w4, bn_scale, bn_bias, bn_mean, bn_var, wq, bq, wk, bk, wv, bv, gamma):
            B, C, H, W = x.shape
            N = H * W
            specs = [(w1, 0, 1), (w2, 6, 6), (w3, 12, 12), (w4, 18, 18)]
            branches = [_bn_relu(_conv(x, w, p, d), bn_scale[i], bn_bias[i], bn_mean[i], bn_var[i]) for i, (w, p, d) in enumerate(specs)]
            x_q = jnp.concatenate(branches, axis=1)
            Q = (jnp.einsum('oi,bihw->bohw', wq[:, :, 0, 0], x_q) + bq[None, :, None, None]).reshape(B, -1, N)
            K = (jnp.einsum('oi,bihw->bohw', wk[:, :, 0, 0], x) + bk[None, :, None, None]).reshape(B, -1, N)
            V = (jnp.einsum('oi,bihw->bohw', wv[:, :, 0, 0], x) + bv[None, :, None, None]).reshape(B, -1, N)
            Qn = _l2n(Q).transpose(0, 2, 1)
            Kn = _l2n(K)
            tailor = 1.0 / (N + jnp.einsum('bnm,bm->bn', Qn, Kn.sum(-1) + EPS))
            vsum = V.sum(-1)[:, :, None]
            mat = jnp.einsum('bmn,bcn->bmc', Kn, V)
            msum = vsum + jnp.einsum('bnm,bmc->bcn', Qn, mat)
            out = (msum * tailor[:, None, :]).reshape(B, C, H, W)
            return gamma * out
        key = jax.random.key(seed)
        ks = jax.random.split(key, 12)
        B, C, H, W = (8, 128, 128, 128)
        M = 16
        d = {'x': jax.random.normal(ks[0], (B, C, H, W), jnp.float32), 'w1': jax.random.normal(ks[1], (32, 128, 1, 1), jnp.float32) * 0.05, 'w2': jax.random.normal(ks[2], (32, 128, 3, 3), jnp.float32) * 0.05, 'w3': jax.random.normal(ks[3], (32, 128, 3, 3), jnp.float32) * 0.05, 'w4': jax.random.normal(ks[4], (32, 128, 3, 3), jnp.float32) * 0.05, 'bn_scale': jnp.ones((4, 32), jnp.float32), 'bn_bias': jnp.zeros((4, 32), jnp.float32), 'bn_mean': jnp.zeros((4, 32), jnp.float32), 'bn_var': jnp.ones((4, 32), jnp.float32), 'wq': jax.random.normal(ks[5], (M, 128, 1, 1), jnp.float32) * 0.05, 'bq': jax.random.normal(ks[6], (M,), jnp.float32) * 0.05, 'wk': jax.random.normal(ks[7], (M, 128, 1, 1), jnp.float32) * 0.05, 'bk': jax.random.normal(ks[8], (M,), jnp.float32) * 0.05, 'wv': jax.random.normal(ks[9], (C, 128, 1, 1), jnp.float32) * 0.05, 'bv': jax.random.normal(ks[10], (C,), jnp.float32) * 0.05, 'gamma': jax.random.uniform(ks[11], (1,), jnp.float32)}
        return d
    _L0_conv_all = _L0_conv_setup()
    _L0_conv_in = {k: v for k, v in _L0_conv_all.items() if k in ('w1', 'w2', 'w3', 'w4', 'bn_scale', 'bn_bias', 'bn_mean', 'bn_var', 'wq', 'bq', 'wk', 'bk', 'wv', 'bv', 'gamma', )}
    del _L0_conv_all

    def _L1_conv_setup():
        import jax, jax.numpy as jnp
        import numpy as np
        D_MODEL = 128
        D_STATE = 16
        D_CONV = 4
        EXPAND = 2
        D_INNER = EXPAND * D_MODEL
        DT_RANK = (D_MODEL + 15) // 16
        BN_EPS = 1e-05
        LRELU_SLOPE = 0.2

        def _mamba(xf, in_proj_w, conv_w, conv_b, x_proj_w, dt_proj_w, dt_proj_b, A_log, Dp, out_proj_w):
            xz = xf @ in_proj_w.T
            xm, z = jnp.split(xz, 2, axis=-1)
            xc = jnp.pad(jnp.transpose(xm, (0, 2, 1)), ((0, 0), (0, 0), (D_CONV - 1, 0)))
            xc = jax.lax.conv_general_dilated(xc, conv_w[:, None, :], (1,), 'VALID', feature_group_count=D_INNER)
            xm = jax.nn.silu(jnp.transpose(xc + conv_b[None, :, None], (0, 2, 1)))
            dbl = xm @ x_proj_w.T
            dtr, Bm, Cm = jnp.split(dbl, [DT_RANK, DT_RANK + D_STATE], axis=-1)
            dt = jax.nn.softplus(dtr @ dt_proj_w.T + dt_proj_b)
            A = -jnp.exp(A_log)
            dA = jnp.exp(dt[..., None] * A)[0]
            dBx = (dt[..., None] * Bm[:, :, None, :] * xm[..., None])[0]

            def step(h, inp):
                dA_t, dBx_t, C_t = inp
                h = dA_t * h + dBx_t
                return (h, h @ C_t)
            h0 = jnp.zeros((D_INNER, D_STATE), xf.dtype)
            _, ys = jax.lax.scan(step, h0, (dA, dBx, Cm[0]))
            y = ys[None] + Dp * xm
            y = y * jax.nn.silu(z)
            return y @ out_proj_w.T
        key = jax.random.key(seed)
        ks = jax.random.split(key, 8)
        s = 0.02
        return {'x': jax.random.normal(ks[0], (1, 128, 128, 128), jnp.float32), 'in_proj_w': jax.random.normal(ks[1], (2 * D_INNER, D_MODEL), jnp.float32) * s, 'conv_w': jax.random.normal(ks[2], (D_INNER, D_CONV), jnp.float32) * s, 'conv_b': jnp.zeros((D_INNER,), jnp.float32), 'x_proj_w': jax.random.normal(ks[3], (DT_RANK + 2 * D_STATE, D_INNER), jnp.float32) * s, 'dt_proj_w': jax.random.normal(ks[4], (D_INNER, DT_RANK), jnp.float32) * s, 'dt_proj_b': jax.random.normal(ks[5], (D_INNER,), jnp.float32) * 0.1, 'A_log': jnp.log(jnp.tile(jnp.arange(1, D_STATE + 1, dtype=jnp.float32), (D_INNER, 1))), 'D': jnp.ones((D_INNER,), jnp.float32), 'out_proj_w': jax.random.normal(ks[6], (D_MODEL, D_INNER), jnp.float32) * s, 'bn_gamma': jnp.ones((D_MODEL,), jnp.float32), 'bn_beta': jnp.zeros((D_MODEL,), jnp.float32)}
    _L1_conv_all = _L1_conv_setup()
    _L1_conv_in = {k: v for k, v in _L1_conv_all.items() if k in ('in_proj_w', 'conv_w', 'conv_b', 'x_proj_w', 'dt_proj_w', 'dt_proj_b', 'A_log', 'D', 'out_proj_w', 'bn_gamma', 'bn_beta', )}
    del _L1_conv_all

    return {
        "x": x,
        "L0_conv_w1": _L0_conv_in["w1"],
        "L0_conv_w2": _L0_conv_in["w2"],
        "L0_conv_w3": _L0_conv_in["w3"],
        "L0_conv_w4": _L0_conv_in["w4"],
        "L0_conv_bn_scale": _L0_conv_in["bn_scale"],
        "L0_conv_bn_bias": _L0_conv_in["bn_bias"],
        "L0_conv_bn_mean": _L0_conv_in["bn_mean"],
        "L0_conv_bn_var": _L0_conv_in["bn_var"],
        "L0_conv_wq": _L0_conv_in["wq"],
        "L0_conv_bq": _L0_conv_in["bq"],
        "L0_conv_wk": _L0_conv_in["wk"],
        "L0_conv_bk": _L0_conv_in["bk"],
        "L0_conv_wv": _L0_conv_in["wv"],
        "L0_conv_bv": _L0_conv_in["bv"],
        "L0_conv_gamma": _L0_conv_in["gamma"],
        "L1_conv_in_proj_w": _L1_conv_in["in_proj_w"],
        "L1_conv_conv_w": _L1_conv_in["conv_w"],
        "L1_conv_conv_b": _L1_conv_in["conv_b"],
        "L1_conv_x_proj_w": _L1_conv_in["x_proj_w"],
        "L1_conv_dt_proj_w": _L1_conv_in["dt_proj_w"],
        "L1_conv_dt_proj_b": _L1_conv_in["dt_proj_b"],
        "L1_conv_A_log": _L1_conv_in["A_log"],
        "L1_conv_D": _L1_conv_in["D"],
        "L1_conv_out_proj_w": _L1_conv_in["out_proj_w"],
        "L1_conv_bn_gamma": _L1_conv_in["bn_gamma"],
        "L1_conv_bn_beta": _L1_conv_in["bn_beta"],
    }

def reference(x, L0_conv_w1, L0_conv_w2, L0_conv_w3, L0_conv_w4, L0_conv_bn_scale, L0_conv_bn_bias, L0_conv_bn_mean, L0_conv_bn_var, L0_conv_wq, L0_conv_bq, L0_conv_wk, L0_conv_bk, L0_conv_wv, L0_conv_bv, L0_conv_gamma, L1_conv_in_proj_w, L1_conv_conv_w, L1_conv_conv_b, L1_conv_x_proj_w, L1_conv_dt_proj_w, L1_conv_dt_proj_b, L1_conv_A_log, L1_conv_D, L1_conv_out_proj_w, L1_conv_bn_gamma, L1_conv_bn_beta):
    import jax
    import jax.numpy as jnp
    def _L0_conv_ref(x, w1, w2, w3, w4, bn_scale, bn_bias, bn_mean, bn_var, wq, bq, wk, bk, wv, bv, gamma):
        import jax, jax.numpy as jnp
        import numpy as np
        BN_EPS = 1e-05
        EPS = 1e-06

        def _conv(x, w, pad, dil):
            return jax.lax.conv_general_dilated(x, w, window_strides=(1, 1), padding=[(pad, pad), (pad, pad)], rhs_dilation=(dil, dil), dimension_numbers=('NCHW', 'OIHW', 'NCHW'))

        def _bn_relu(x, s, b, m, v):
            inv = (s / jnp.sqrt(v + BN_EPS))[None, :, None, None]
            return jax.nn.relu((x - m[None, :, None, None]) * inv + b[None, :, None, None])

        def _l2n(x):
            return x / jnp.linalg.norm(x, axis=1, keepdims=True)

        def _forward(x, w1, w2, w3, w4, bn_scale, bn_bias, bn_mean, bn_var, wq, bq, wk, bk, wv, bv, gamma):
            B, C, H, W = x.shape
            N = H * W
            specs = [(w1, 0, 1), (w2, 6, 6), (w3, 12, 12), (w4, 18, 18)]
            branches = [_bn_relu(_conv(x, w, p, d), bn_scale[i], bn_bias[i], bn_mean[i], bn_var[i]) for i, (w, p, d) in enumerate(specs)]
            x_q = jnp.concatenate(branches, axis=1)
            Q = (jnp.einsum('oi,bihw->bohw', wq[:, :, 0, 0], x_q) + bq[None, :, None, None]).reshape(B, -1, N)
            K = (jnp.einsum('oi,bihw->bohw', wk[:, :, 0, 0], x) + bk[None, :, None, None]).reshape(B, -1, N)
            V = (jnp.einsum('oi,bihw->bohw', wv[:, :, 0, 0], x) + bv[None, :, None, None]).reshape(B, -1, N)
            Qn = _l2n(Q).transpose(0, 2, 1)
            Kn = _l2n(K)
            tailor = 1.0 / (N + jnp.einsum('bnm,bm->bn', Qn, Kn.sum(-1) + EPS))
            vsum = V.sum(-1)[:, :, None]
            mat = jnp.einsum('bmn,bcn->bmc', Kn, V)
            msum = vsum + jnp.einsum('bnm,bmc->bcn', Qn, mat)
            out = (msum * tailor[:, None, :]).reshape(B, C, H, W)
            return gamma * out
        return _forward(x, w1, w2, w3, w4, bn_scale, bn_bias, bn_mean, bn_var, wq, bq, wk, bk, wv, bv, gamma)

    def _L1_conv_ref(x, in_proj_w, conv_w, conv_b, x_proj_w, dt_proj_w, dt_proj_b, A_log, D, out_proj_w, bn_gamma, bn_beta):
        import jax, jax.numpy as jnp
        import numpy as np
        D_MODEL = 128
        D_STATE = 16
        D_CONV = 4
        EXPAND = 2
        D_INNER = EXPAND * D_MODEL
        DT_RANK = (D_MODEL + 15) // 16
        BN_EPS = 1e-05
        LRELU_SLOPE = 0.2

        def _mamba(xf, in_proj_w, conv_w, conv_b, x_proj_w, dt_proj_w, dt_proj_b, A_log, Dp, out_proj_w):
            xz = xf @ in_proj_w.T
            xm, z = jnp.split(xz, 2, axis=-1)
            xc = jnp.pad(jnp.transpose(xm, (0, 2, 1)), ((0, 0), (0, 0), (D_CONV - 1, 0)))
            xc = jax.lax.conv_general_dilated(xc, conv_w[:, None, :], (1,), 'VALID', feature_group_count=D_INNER)
            xm = jax.nn.silu(jnp.transpose(xc + conv_b[None, :, None], (0, 2, 1)))
            dbl = xm @ x_proj_w.T
            dtr, Bm, Cm = jnp.split(dbl, [DT_RANK, DT_RANK + D_STATE], axis=-1)
            dt = jax.nn.softplus(dtr @ dt_proj_w.T + dt_proj_b)
            A = -jnp.exp(A_log)
            dA = jnp.exp(dt[..., None] * A)[0]
            dBx = (dt[..., None] * Bm[:, :, None, :] * xm[..., None])[0]

            def step(h, inp):
                dA_t, dBx_t, C_t = inp
                h = dA_t * h + dBx_t
                return (h, h @ C_t)
            h0 = jnp.zeros((D_INNER, D_STATE), xf.dtype)
            _, ys = jax.lax.scan(step, h0, (dA, dBx, Cm[0]))
            y = ys[None] + Dp * xm
            y = y * jax.nn.silu(z)
            return y @ out_proj_w.T
        B, C, H, W = x.shape
        xf = jnp.transpose(x, (0, 2, 3, 1)).reshape(1, B * H * W, C)
        xf = _mamba(xf, in_proj_w, conv_w, conv_b, x_proj_w, dt_proj_w, dt_proj_b, A_log, D, out_proj_w)
        xr = jnp.transpose(xf.reshape(B, H, W, C), (0, 3, 1, 2))
        mu = xr.mean((0, 2, 3), keepdims=True)
        var = xr.var((0, 2, 3), keepdims=True)
        xn = (xr - mu) / jnp.sqrt(var + BN_EPS)
        xn = xn * bn_gamma[None, :, None, None] + bn_beta[None, :, None, None]
        xp = jnp.where(xn > 0, xn, LRELU_SLOPE * xn)
        return xp + x

    def _gn(v, G=32, eps=1e-5):
        B_, C_, H_, W_ = v.shape
        g = v.reshape(B_, G, C_ // G, H_, W_)
        m = jnp.mean(g, axis=(2, 3, 4), keepdims=True)
        s = jnp.var(g, axis=(2, 3, 4), keepdims=True)
        return ((g - m) / jnp.sqrt(s + eps)).reshape(v.shape)

    def _ln_c(v, eps=1e-6):
        m = jnp.mean(v, axis=1, keepdims=True)
        s = jnp.var(v, axis=1, keepdims=True)
        return (v - m) / jnp.sqrt(s + eps)

    def _ln_t(v, eps=1e-5):
        m = jnp.mean(v, axis=-1, keepdims=True)
        s = jnp.var(v, axis=-1, keepdims=True)
        return (v - m) / jnp.sqrt(s + eps)

    def _to_tokens(v):
        B_, C_, H_, W_ = v.shape
        return v.reshape(B_, C_, H_ * W_).transpose(0, 2, 1)
    def _from_tokens(t, like):
        B_, C_, H_, W_ = like.shape
        return t.transpose(0, 2, 1).reshape(B_, C_, H_, W_)

    x = _L0_conv_ref(x, L0_conv_w1, L0_conv_w2, L0_conv_w3, L0_conv_w4, L0_conv_bn_scale, L0_conv_bn_bias, L0_conv_bn_mean, L0_conv_bn_var, L0_conv_wq, L0_conv_bq, L0_conv_wk, L0_conv_bk, L0_conv_wv, L0_conv_bv, L0_conv_gamma)
    x = _L1_conv_ref(x, L1_conv_in_proj_w, L1_conv_conv_w, L1_conv_conv_b, L1_conv_x_proj_w, L1_conv_dt_proj_w, L1_conv_dt_proj_b, L1_conv_A_log, L1_conv_D, L1_conv_out_proj_w, L1_conv_bn_gamma, L1_conv_bn_beta)
    return x


_drawn_inputs = setup_inputs


def setup_inputs(seed=0):
    import zlib

    import numpy as np

    out = dict(_drawn_inputs(seed))
    spreads = {'L0_conv_bn_scale': (1.0, 0.6),
     'L0_conv_bn_bias': (0.0, 2.0),
     'L0_conv_bn_mean': (0.0, 2.0),
     'L0_conv_bn_var': (1.0, 0.6),
     'L1_conv_conv_b': (0.0, 0.1),
     'L1_conv_D': (1.0, 0.6),
     'L1_conv_bn_gamma': (1.0, 0.6),
     'L1_conv_bn_beta': (0.0, 0.1)}
    factors = {'L0_conv_w1': 3.832,
     'L0_conv_bq': 8.0,
     'L0_conv_bk': 34.567,
     'L1_conv_conv_w': 64.0,
     'L1_conv_x_proj_w': 64.0,
     'L1_conv_dt_proj_w': 64.0,
     'L1_conv_dt_proj_b': 64.0,
     'L1_conv_A_log': 64.0}
    for name, (base, spread) in spreads.items():
        noise = np.random.default_rng([zlib.crc32(name.encode()), seed]).standard_normal(out[name].shape)
        drawn = base * np.exp(spread * noise) if base else spread * noise
        out[name] = jnp.asarray(drawn.astype(out[name].dtype))
    for name, factor in factors.items():
        out[name] = (out[name] * factor).astype(out[name].dtype)
    return out
```

```python
import numpy as np
import concourse.bass as bass
from concourse import mybir
from contextlib import ExitStack

B, C, H, W = 8, 128, 128, 128
N = H * W
PAD = 18
HP, WP = H + 2 * PAD, W + 2 * PAD
M = 16
F = M + 1
TAPS = 4
DI = 256
HALVES = DI // 128
S = 16
RANK = 8
CH = 512
ROWS = CH // W
TILES = CH // 128
WIN_CH = 2
WIN_ROWS = WIN_CH * ROWS + 2 * PAD
BODY = 4
IMG_CH = N // CH
BODIES = IMG_CH // BODY
CHUNKS = B * IMG_CH
GRP = 4
GROUPS = S // GRP
UNITS = GROUPS * HALVES
SEG = CH + 1
BN_EPS, NORM_EPS = 1e-5, 1e-6
LOG_MAX = 82.9
FIN = 2048
BC3 = 3 * 2 * S
DIL = (6, 12, 18)
CREDIT = 32


def after(item):
    return item + 1 + CREDIT


def program(nc, t, out):
    f32, bf16 = mybir.dt.float32, mybir.dt.bfloat16
    ALU, ACT, AX = mybir.AluOpType, mybir.ActivationFunctionType, mybir.AxisListType
    ctx = ExitStack()
    with ctx:
        def sb(name, shape, dt=f32):
            return ctx.enter_context(nc.sbuf_tensor(name, shape, dt))

        def sem(name):
            return ctx.enter_context(nc.semaphore(name))

        xr_scr = nc.dram_tensor("xr_scr", (128, CHUNKS * CH), f32).ap()
        g_scr = nc.dram_tensor("g_scr", (F, CHUNKS * CH), f32).ap()

        ident = sb("ident", [128, 128])
        ones = sb("ones", [128, 128])
        onehot = sb("onehot", [BC3, 2 * S, 128], bf16)
        w_taps = sb("w_taps", [128, 27, 32])
        w_mid = sb("w_mid", [128, 128])
        bn4 = sb("bn4", [128, 4])
        bn_s, bn_b, bn_m, bn_v = (bn4[:, k:k + 1] for k in range(4))
        bn_tmp = sb("bn_tmp", [128, 4])
        wq = sb("wq", [128, M])
        xk_rhs = sb("xk_rhs", [128, 128 + M])
        bq_b = sb("bq_b", [128, M])
        bk_b = sb("bk_b", [128, M])
        wv = sb("wv", [128, 128])
        bv = sb("bv", [1, 128])
        gamma = sb("gamma", [128, 1])
        w_in = sb("w_in", [128, 2 * DI])
        conv_mask = sb("conv_mask", [128, 2 * DI])
        conv_b = sb("conv_b", [128, HALVES])
        x_proj = sb("x_proj", [128, HALVES, BC3 + RANK])
        dt_w = sb("dt_w", [128, DI])
        dt_b = sb("dt_b", [128, HALVES])
        A = sb("A", [128, HALVES, S])
        Dp = sb("Dp", [128, HALVES])
        w_out = sb("w_out", [128, HALVES, 128])
        bn2 = sb("bn2", [128, 2])

        shared = sb("shared", [128, 8 * GRP * SEG])
        xw = [shared[:, p * WIN_ROWS * WP:(p + 1) * WIN_ROWS * WP].rearrange("c (r w) -> c r w", w=WP)
              for p in range(2)]
        decay = [shared[:, s * GRP * SEG:(s + 1) * GRP * SEG] for s in range(4)]
        state = [shared[:, (4 + s) * GRP * SEG:(5 + s) * GRP * SEG] for s in range(4)]

        def by_state(unit):
            return unit.rearrange("c (n t) -> c n t", t=SEG)

        keys = sb("keys", [128, TILES, M])
        keys_sq = sb("keys_sq", [128, TILES, M])
        knorm = sb("knorm", [128, TILES])
        kn = sb("kn", [128, 2, TILES, F])
        q_raw = sb("q_raw", [128, N // 128, M])
        g_t = sb("g_t", [128, N // 128, F])
        sums = sb("sums", [128, 2 * F])
        ksum_b = sb("ksum_b", [128, M])
        qnorm = sb("qnorm", [128, N // 128])
        qk = sb("qk", [128, N // 128])
        mv_t4 = sb("mv_t4", [128, TAPS, 32])
        mv_all = sb("mv_all", [F, B, 128])
        mv_now = sb("mv_now", [F, 128])
        w_xz = sb("w_xz", [128, 2 * DI])
        w_edge = sb("w_edge", [128, DI])

        g_rep = sb("g_rep", [128, TILES, TAPS, 32])
        g = sb("g", [128, 2, CH + TAPS - 1])
        xm = sb("xm", [128, 2, HALVES, CH])
        zs = sb("zs", [128, 2, HALVES, CH])
        dbl = sb("dbl", [BC3 + RANK, CH])
        resid = sb("resid", [64, CH])
        parts = sb("parts", [BC3, 2, CH], bf16)
        sp_e = sb("sp_e", [128, HALVES, CH])
        sp_w = sb("sp_w", [128, HALVES, CH])
        sp_c = sb("sp_c", [128, HALVES, CH])
        sp_r = sb("sp_r", [128, HALVES, CH])
        dt = sb("dt", [128, 2, HALVES, CH])
        u = sb("u", [128, 2, HALVES, CH])
        c_sb = sb("c_sb", [128, 2, GRP, CH])
        sq_tmp = c_sb[:, 0, :, :].rearrange("p n t -> p (n t)").rearrange("p (a m) -> p a m", m=M)
        carry = sb("carry", [128, UNITS, GRP])
        yt = sb("yt", [128, HALVES, CH])
        xr = sb("xr", [128, 2, CH])
        y_relu = yt
        x_t = sp_e[:, :, :].rearrange("p a (b c) -> p a b c", c=128)
        stats = sb("stats", [128, CHUNKS, 6])
        mom = sb("mom", [128, 4])

        bank = [ctx.enter_context(nc.psum_tensor(f"bank{k}", [128, CH], f32)) for k in range(2)]
        b_ps = ctx.enter_context(nc.psum_tensor("b_ps", [128, GRP, CH], f32))
        ycur = [ctx.enter_context(nc.psum_tensor(f"ycur{k}", [128, CH], f32)) for k in range(2)]
        fe, c_ps = bank
        conv_ps = [b_ps[:, k, :] for k in range(2)]
        xk_ps = [b_ps[:, 2 + k, 0:2 * (128 + M)].rearrange("p (a n) -> p a n", a=2) for k in range(2)]
        q_ps = ycur[0][:, 0:TILES * M]
        s_ps = ycur[1][:, 0:2 * F]

        fin_x = [shared[:, p * FIN:(p + 1) * FIN] for p in range(2)]
        fin_g = [shared[0:F, (2 + p) * FIN:(3 + p) * FIN] for p in range(2)]
        fin_y = [shared[:, (4 + p) * FIN:(5 + p) * FIN] for p in range(2)]

        loaded = sem("loaded")
        win_loaded = [sem(f"win_loaded{p}") for p in range(2)]
        feat_stored = [sem(f"feat_stored{p}") for p in range(2)]
        xr_stored = [sem(f"xr_stored{p}") for p in range(2)]
        fin_loaded = [sem(f"fin_loaded{p}") for p in range(2)]
        out_stored = [sem(f"out_stored{p}") for p in range(2)]
        counting = {}
        for who, names in {
            "tensor": "conv_done xk_done s_done q_done mvt_done mv_done p4_done gt_done xz_done dbl_done "
                      "dtm_done b_done c_done summed outp_done fin_mm img_pe".split(),
            "vector": "dve_setup k_taken k_sq k_red kn_ready q_taken s_taken k_done ksb_ready qf1 qf2 qf3 qf4 gt_ready mvt_ready "
                      "mv_ready w_ready g_rep_ready split1 split2 split3 split4 parts_ready sp1 sp2 sp3 sp4 dt_ready "
                      "u_ready filled b_used scanned carried y_taken y1 gated stat_done edge_ready mom1 mom2 "
                      "mom_ready fin_v fin_done mvnow_ready cleared".split(),
            "scalar": "act_setup relu_done xt_ready lnk rk_ready qn_ready g_copied xm_ready z_ready dbl_ready sp_lin sp_abs "
                      "sp_exp sp_ln decay_ready c_ready xr_ready std_ready fin_a".split(),
            "gpsimd": "weighted".split(),
        }.items():
            for name in names:
                counting[name] = sem(name)
                counting.setdefault(who, []).append(counting[name])
        s = counting

        block = ctx.enter_context(nc.Block())

        def raise_credit(e, who):
            for x in s[who]:
                e.sem_inc(x, CREDIT)

        @block.sync
        def _(sp):
            for p in range(2):
                sp.sem_inc(feat_stored[p], 16)
                sp.sem_inc(xr_stored[p], 16)
                sp.sem_inc(out_stored[p], 16)
            bn = [(bn4[:, k:k + 1], t[n]) for k, n in enumerate(("bn_scale", "bn_bias", "bn_mean", "bn_var"))]
            loads = bn + [
                (ident[:, :], t["ident"]), (onehot[:, :, :], t["onehot"]), (w_taps[:, :, :], t["w_taps"]),
                (w_mid[:, :], t["w_mid"]), (wq[:, :], t["wq"]), (xk_rhs[:, 0:128], t["ident"]),
                (xk_rhs[:, 128:], t["wk"]), (bq_b[:, :], t["bq"].broadcast_to([128, M])),
                (bk_b[:, :], t["bk"].broadcast_to([128, M])), (wv[:, :], t["wv"]), (bv[:, :], t["bv"]),
                (gamma[:, :], t["gamma"].broadcast_to([128, 1])), (w_in[:, :], t["w_in"]),
                (conv_b[:, :], t["conv_b"]), (x_proj[:, :, :], t["x_proj"]), (dt_w[BC3:BC3 + RANK, :], t["dt_w"]),
                (dt_b[:, :], t["dt_b"]), (A[:, :, :], t["A_log"]), (Dp[:, :], t["D"]),
                (w_out[:, :, :], t["w_out"]), (bn2[:, 0:1], t["bn_gamma"]), (bn2[:, 1:2], t["bn_beta"]),
            ]
            sp.wait_ge(s["dve_setup"], after(0))
            loads += [(conv_mask[32 * k:32 * k + F, 0:DI], t["conv_w"][k:k + 1, :].broadcast_to([F, DI]))
                      for k in range(TAPS)]
            assert len(loads) == N_LOADS
            for dst, src in loads:
                sp.dma_start(dst, src).then_inc(loaded, 16)

            def windows(img, w):
                sp.wait_ge(s["img_pe"], img + CREDIT)
                for p in range(2):
                    sp.wait_ge(s["conv_done"], after(img * IMG_CH + w * BODY + (p - 2) * WIN_CH + (WIN_CH - 1)))
                    row = w * (2 * WIN_CH * ROWS) + p * WIN_CH * ROWS
                    sp.dma_start(xw[p], t["x"][bass.ds(img, 1), :, bass.ds(row, WIN_ROWS), :]
                                 .rearrange("a c r w -> (a c) r w")).then_inc(win_loaded[p], 16)

            def store_features(f, par):
                sp.wait_ge(s["g_copied"], after(f))
                sp.dma_start(g_scr[:, bass.ds(f * CH, CH)], g[96:96 + F, par, 0:CH]).then_inc(feat_stored[par], 16)

            def store_xr(q, par):
                sp.wait_ge(s["xr_ready"], after(q))
                sp.dma_start(xr_scr[:, bass.ds(q * CH, CH)], xr[:, par, :]).then_inc(xr_stored[par], 16)

            def body(q0, first=False, last=False):
                for j in range(BODY):
                    if not (first and j == 0):
                        store_xr(q0 + (j - 1), (j - 1) % 2)
                    if not (last and j == BODY - 1):
                        store_features(q0 + (j + 1), (j + 1) % 2)
                if last:
                    store_xr(q0 + (BODY - 1), (BODY - 1) % 2)

            with sp.Fori(0, B) as img:
                with sp.Fori(0, BODIES) as w:
                    windows(img, w)
                store_features(img * IMG_CH, 0)
                body(img * IMG_CH, first=True)
                with sp.Fori(1, BODIES - 1) as w:
                    body(img * IMG_CH + w * BODY)
                body(img * IMG_CH + (IMG_CH - BODY), last=True)

            for p in range(2):
                sp.wait_ge(feat_stored[p], 16 + 16 * (CHUNKS // 2))
                sp.wait_ge(xr_stored[p], 16 + 16 * (CHUNKS // 2))
            sp.wait_ge(s["img_pe"], B + CREDIT)
            sp.wait_ge(s["stat_done"], after(CHUNKS - 1))
            with sp.Fori(0, B) as img:
                with sp.Fori(0, N // (2 * FIN)) as w:
                    for p in range(2):
                        it = img * (N // FIN) + w * 2 + p
                        sp.wait_ge(s["fin_done"], after(it - 2))
                        sp.wait_ge(s["fin_mm"], after(it - 2))
                        sp.dma_start(fin_x[p], xr_scr[:, bass.ds(it * FIN, FIN)]).then_inc(fin_loaded[p], 16)
                        sp.dma_start(fin_g[p], g_scr[:, bass.ds(it * FIN, FIN)]).then_inc(fin_loaded[p], 16)
            for p in range(2):
                sp.wait_ge(out_stored[p], 16 + 16 * (B * N // FIN // 2))


        @block.tensor
        def _(pe):
            raise_credit(pe, "tensor")
            pe.wait_ge(loaded, 16 * N_LOADS)
            pe.wait_ge(s["dve_setup"], after(1))

            def layer0_chunk(img, w, j):
                q = img * IMG_CH + w * BODY + j
                p, r0 = j // WIN_CH, PAD + (j % WIN_CH) * ROWS
                if j % WIN_CH == 0:
                    pe.wait_ge(win_loaded[p], (img * BODIES + w) * 16 + 16)
                for pair in range(2):
                    pe.wait_ge(s["xt_ready"], after(q * 2 + (pair - 2)))
                    pe.wait_ge(s["k_taken"], after(q * 2 + (pair - 2)))
                    for a in range(2):
                        tile = nc.tensor.matmul(xk_ps[pair][:, a, :], xw[p][:, r0 + 2 * pair + a, PAD:PAD + W],
                                                xk_rhs[:, :], start=True, stop=True)
                    tile.then_inc(s["xk_done"], 1)
                pe.wait_ge(s["relu_done"], after(q - 2))
                dst = conv_ps[j % 2]
                nc.tensor.matmul(dst, w_mid[:, :], xw[p][:, r0:r0 + ROWS, PAD:PAD + W], start=True, stop=True)
                taps = [(k, b) for k in range(9) if k != 4 for b in range(3)]
                for k, b in taps:
                    y0, x0 = r0 + (k // 3 - 1) * DIL[b], PAD + (k % 3 - 1) * DIL[b]
                    tap = nc.tensor.matmul(dst[32 * b + 32:32 * b + 64, :], w_taps[:, 9 * b + k, :],
                                           xw[p][:, y0:y0 + ROWS, x0:x0 + W], start=False,
                                           stop=True, skip_group_check=True)
                tap.then_inc(s["conv_done"], 1)
                pe.wait_ge(s["kn_ready"], after(q))
                pe.wait_ge(s["xt_ready"], after(q * 2 + 1))
                pe.wait_ge(s["s_taken"], after(q - 1))
                for a in range(TILES):
                    nc.tensor.matmul(s_ps[:, 0:F], x_t[:, j % 2, a, :], kn[:, j % 2, a, :],
                                     start=a == 0, stop=a == TILES - 1)
                for a in range(TILES):
                    tile = nc.tensor.matmul(s_ps[:, F:2 * F], ones[:, :], kn[:, j % 2, a, :],
                                            start=a == 0, stop=a == TILES - 1)
                tile.then_inc(s["s_done"], 1)
                pe.wait_ge(s["relu_done"], after(q))
                pe.wait_ge(s["q_taken"], after(q - 1))
                for a in range(TILES):
                    tile = nc.tensor.matmul(q_ps[:, a * M:(a + 1) * M], y_relu[:, j % 2, a * 128:(a + 1) * 128],
                                            wq[:, :], start=True, stop=True)
                tile.then_inc(s["q_done"], 1)

            def image_weights(img):
                pe.wait_ge(s["ksb_ready"], after(img))
                nc.tensor.matmul(fe[:, 0:F], wv[:, :], sums[:, 0:F], start=True, stop=False)
                nc.tensor.matmul(fe[:, 0:F], bv[0:1, :], sums[0:1, F:2 * F], start=False, stop=True) \
                    .then_inc(s["mvt_done"], 1)
                pe.wait_ge(s["c_ready"], after(img * (IMG_CH * S) - 1))
                nc.tensor.matmul(c_ps[0:F, 0:128], sums[:, 0:F], wv[:, :], start=True, stop=False)
                nc.tensor.matmul(c_ps[0:F, 0:128], sums[0:1, F:2 * F], bv[0:1, :], start=False, stop=True) \
                    .then_inc(s["mv_done"], 1)
                pe.wait_ge(s["mvt_ready"], after(img))
                nc.tensor.matmul(ycur[0][:, :], mv_t4[:, :, :].rearrange("p k m -> p (k m)"), w_in[:, :],
                                 start=True, stop=True).then_inc(s["p4_done"], 1)

            def features(f):
                pe.wait_ge(s["g_rep_ready"], after(f))
                for a in range(TILES):
                    tile = nc.tensor.matmul(fe[:, a * 128:(a + 1) * 128],
                                            g_rep[:, a, :, :].rearrange("p k m -> p (k m)"), ident[:, :],
                                            start=True, stop=True)
                tile.then_inc(s["gt_done"], 1)

            def project_in(f, par):
                pe.wait_ge(s["g_copied"], after(f))
                for k in range(2 * HALVES):
                    if k:
                        pe.wait_ge(s["xm_ready" if k <= 2 else "z_ready"],
                                   after(f * 2 + (k - 1) if k <= 2 else f * 2 + (k - 3)))
                    edge = k < HALVES
                    last = nc.tensor.matmul(fe[:, :], w_xz[:, k * 128:(k + 1) * 128], g[:, par, 0:CH],
                                            start=True, stop=True)
                    if edge:
                        last = nc.tensor.matmul(fe[:, 0:TAPS - 1], w_edge[:, k * 128:(k + 1) * 128],
                                                g[:, 1 - par, CH:CH + TAPS - 1], start=False, stop=True,
                                                skip_group_check=True)
                    last.then_inc(s["xz_done"], 1)

            def project_x(f, par):
                pe.wait_ge(s["z_ready"], after(f * 2 + 1))
                for h in range(HALVES):
                    last = nc.tensor.matmul(fe[0:BC3 + RANK, :], x_proj[:, h, :], xm[:, par, h, :],
                                            start=h == 0, stop=h == 1)
                last.then_inc(s["dbl_done"], 1)

            def project_dt(f):
                pe.wait_ge(s["dbl_ready"], after(f))
                for h in range(HALVES):
                    if h:
                        pe.wait_ge(s["sp_lin"], after(f * 2))
                    nc.tensor.matmul(fe[:, :], dt_w[BC3:BC3 + RANK, h * 128:(h + 1) * 128],
                                     dbl[BC3:BC3 + RANK, :], start=True, stop=True).then_inc(s["dtm_done"], 1)
                pe.wait_ge(s["sp_lin"], after(f * 2 + 1))

            def spread(q, grp, par):
                if grp == 0:
                    pe.wait_ge(s["parts_ready"], after(q))
                pe.wait_ge(s["b_used"], after(q * GROUPS + (grp - 1)))
                for i in range(GRP):
                    last = nc.tensor.matmul(b_ps[:, i, :], onehot[:, grp * GRP + i, :], parts[:, par, :],
                                            start=True, stop=True)
                last.then_inc(s["b_done"], 1)
                for i in range(GRP):
                    pe.wait_ge(s["c_ready"], after(q * S + (grp * GRP + i - 1)))
                    nc.tensor.matmul(c_ps[:, :], onehot[:, S + grp * GRP + i, :], parts[:, par, :],
                                     start=True, stop=True).then_inc(s["c_done"], 1)

            def sum_group(q, grp):
                for h in range(HALVES):
                    pe.wait_ge(s["weighted"], after(q * UNITS + (2 * grp + h)))
                    if grp == 0:
                        pe.wait_ge(s["y_taken"], after(q * 2 + (h - 2)))
                    unit = by_state(state[2 * (grp % 2) + h])
                    for i in range(GRP):
                        last = nc.tensor.matmul(ycur[h][:, :], ident[:, :], unit[:, i, 1:SEG],
                                                start=grp == 0 and i == 0, stop=grp == GROUPS - 1 and i == GRP - 1)
                    last.then_inc(s["summed"], 1)

            def project_out(q):
                pe.wait_ge(s["gated"], after(q))
                for h in range(HALVES):
                    last = nc.tensor.matmul(fe[:, :], w_out[:, h, :], yt[:, h, :], start=h == 0, stop=h == 1)
                last.then_inc(s["outp_done"], 1)

            def body(q0, first=False, last=False):
                for j in range(BODY):
                    q, f = q0 + j, q0 + (j + 1)
                    prev, ahead = not (first and j == 0), not (last and j == BODY - 1)
                    for grp in range(GROUPS):
                        spread(q, grp, j % 2)
                        if grp:
                            sum_group(q, grp - 1)
                        elif prev:
                            sum_group(q - 1, GROUPS - 1)
                        if grp == 0 and ahead:
                            features(f)
                        if grp == 1:
                            if ahead:
                                project_in(f, (j + 1) % 2)
                                project_x(f, (j + 1) % 2)
                        if grp == 2:
                            if ahead:
                                project_dt(f)
                            if prev:
                                project_out(q - 1)
                                pe.wait_ge(s["xr_ready"], after(q - 1))
                if last:
                    q = q0 + (BODY - 1)
                    sum_group(q, GROUPS - 1)
                    project_out(q)

            with pe.Fori(0, B) as img:
                with pe.Fori(0, BODIES) as w:
                    for j in range(BODY):
                        layer0_chunk(img, w, j)
                image_weights(img)
                f0 = img * IMG_CH
                pe.wait_ge(s["w_ready"], after(img))
                pe.wait_ge(s["mv_ready"], after(img))
                features(f0)
                project_in(f0, 0)
                project_x(f0, 0)
                project_dt(f0)
                pe.wait_ge(s["edge_ready"], after(img))
                body(f0, first=True)
                with pe.Fori(1, BODIES - 1) as w:
                    body(img * IMG_CH + w * BODY)
                body(img * IMG_CH + (IMG_CH - BODY), last=True)
                pe.wait_ge(s["xr_ready"], after(img * IMG_CH + (IMG_CH - 1)))
                pe.sem_inc(s["img_pe"], 1)

            with pe.Fori(0, B) as img:
                with pe.Fori(0, N // (2 * FIN)) as w:
                    pe.wait_ge(s["mvnow_ready"], after(img))
                    for p in range(2):
                        it = img * (N // FIN) + w * 2 + p
                        pe.wait_ge(fin_loaded[p], (img * (N // FIN // 2) + w) * 32 + 32)
                        pe.wait_ge(s["fin_v"], after(it - 1))
                        for i in range(FIN // CH):
                            last = nc.tensor.matmul(b_ps[:, i, :], mv_now[:, :], fin_g[p][:, i * CH:(i + 1) * CH],
                                                    start=True, stop=True)
                        last.then_inc(s["fin_mm"], 1)

        @block.scalar
        def _(act):
            raise_credit(act, "scalar")
            act.wait_ge(loaded, 16 * N_LOADS)
            act.wait_ge(s["dve_setup"], after(2))
            nc.scalar.activation(bn_tmp[:, 1:2], bn_tmp[:, 0:1], ACT.Sqrt).then_inc(s["act_setup"], 1)
            nc.scalar.activation(A[:, :, :], A[:, :, :], ACT.Exp).then_inc(s["act_setup"], 1)
            act.wait_ge(s["dve_setup"], after(3))

            def layer0_chunk(img, w, j):
                q = img * IMG_CH + w * BODY + j
                for pair in range(2):
                    act.wait_ge(s["xk_done"], after(q * 2 + pair))
                    act.wait_ge(s["s_done"], after(q - 2))
                    nc.scalar.activation(x_t[:, j % 2, 2 * pair:2 * pair + 2, :], xk_ps[pair][:, :, 0:128],
                                         ACT.Copy).then_inc(s["xt_ready"], 1)
                act.wait_ge(s["k_red"], after(q))
                nc.scalar.activation(knorm[:, :], knorm[:, :], ACT.Ln).then_inc(s["lnk"], 1)
                act.wait_ge(s["lnk"], after(q))
                nc.scalar.activation(knorm[:, :], knorm[:, :], ACT.Exp, scale=-0.5).then_inc(s["rk_ready"], 1)
                act.wait_ge(s["conv_done"], after(q))
                act.wait_ge(s["q_done"], after(q - 2))
                nc.scalar.activation(y_relu[:, j % 2, :], conv_ps[j % 2], ACT.Relu, bias=bn_tmp[:, 3:4],
                                     scale=bn_tmp[:, 2:3]).then_inc(s["relu_done"], 1)

            def features(f, par):
                act.wait_ge(s["gt_done"], after(f))
                act.wait_ge(feat_stored[par], (f - par) * 8 + 16)
                act.wait_ge(s["xz_done"], after(f * 4 - 1))
                for k in range(TAPS):
                    shift = TAPS - 1 - k
                    last = nc.scalar.activation(g[32 * k:32 * k + 32, par, shift:shift + CH],
                                                fe[32 * k:32 * k + 32, :], ACT.Copy)
                last.then_inc(s["g_copied"], 1)

            def silus(f, par):
                act.wait_ge(s["gated"], after(f - 2))
                for k in range(2 * HALVES):
                    act.wait_ge(s["xz_done"], after(f * 4 + k))
                    if k < HALVES:
                        nc.scalar.activation(xm[:, par, k, :], fe[:, :], ACT.Silu, bias=conv_b[:, k:k + 1]) \
                            .then_inc(s["xm_ready"], 1)
                    else:
                        nc.scalar.activation(zs[:, par, k - HALVES, :], fe[:, :], ACT.Silu).then_inc(s["z_ready"], 1)

            def take_dbl(f):
                act.wait_ge(s["dbl_done"], after(f))
                act.wait_ge(s["dtm_done"], after(f * 2 - 1))
                act.wait_ge(s["parts_ready"], after(f - 1))
                nc.scalar.activation(dbl[:, :], fe[0:BC3 + RANK, :], ACT.Copy).then_inc(s["dbl_ready"], 1)

            def softplus_start(f):
                act.wait_ge(s["dt_ready"], after(f - 1))
                for h in range(HALVES):
                    act.wait_ge(s["dtm_done"], after(f * 2 + h))
                    nc.scalar.activation(sp_e[:, h, :], fe[:, :], ACT.Abs, bias=dt_b[:, h:h + 1]) \
                        .then_inc(s["sp_abs"], 1)
                    nc.scalar.activation(sp_r[:, h, :], fe[:, :], ACT.Relu, bias=dt_b[:, h:h + 1]) \
                        .then_inc(s["sp_lin"], 1)
                act.wait_ge(s["sp_abs"], after(f * 2 + 1))
                nc.scalar.activation(sp_e[:, :, :], sp_e[:, :, :], ACT.Exp, scale=-1.0).then_inc(s["sp_exp"], 1)

            def softplus_log(f):
                act.wait_ge(s["sp2"], after(f))
                nc.scalar.activation(sp_w[:, :, :], sp_w[:, :, :], ACT.Ln).then_inc(s["sp_ln"], 1)

            def decays(q, grp, par):
                for h in range(HALVES):
                    k = 2 * grp + h
                    if grp == 0 and h == 0:
                        act.wait_ge(s["dt_ready"], after(q))
                    act.wait_ge(s["scanned"], after(q * UNITS + (k - 4)))
                    unit = by_state(decay[2 * (grp % 2) + h])
                    for i in range(GRP):
                        n = grp * GRP + i
                        last = nc.scalar.activation(unit[:, i, 1:SEG], dt[:, par, h, :], ACT.Exp,
                                                    scale=A[:, h, n:n + 1])
                    last.then_inc(s["decay_ready"], 1)

            def take_c(q, grp):
                act.wait_ge(s["weighted"], after(q * UNITS + (2 * grp - 3)))
                for i in range(GRP):
                    act.wait_ge(s["c_done"], after(q * S + (grp * GRP + i)))
                    nc.scalar.activation(c_sb[:, grp % 2, i, :], c_ps[:, :], ACT.Copy).then_inc(s["c_ready"], 1)

            def take_out(q, par):
                act.wait_ge(s["outp_done"], after(q))
                act.wait_ge(xr_stored[par], (q - par) * 8 + 16)
                act.wait_ge(s["stat_done"], after(q - 2))
                nc.scalar.activation(xr[:, par, :], fe[:, :], ACT.Copy).then_inc(s["xr_ready"], 1)

            def body(q0, first=False, last=False):
                for j in range(BODY):
                    q, f = q0 + j, q0 + (j + 1)
                    prev, ahead = not (first and j == 0), not (last and j == BODY - 1)
                    for grp in range(GROUPS):
                        decays(q, grp, j % 2)
                        take_c(q, grp)
                        if grp == 0 and ahead:
                            features(f, (j + 1) % 2)
                        if grp == 1 and ahead:
                            silus(f, (j + 1) % 2)
                            take_dbl(f)
                        if grp == 2:
                            if ahead:
                                softplus_start(f)
                            if prev:
                                take_out(q - 1, (j - 1) % 2)
                    if ahead:
                        softplus_log(f)
                if last:
                    take_out(q0 + (BODY - 1), (BODY - 1) % 2)

            with act.Fori(0, B) as img:
                with act.Fori(0, BODIES) as w:
                    for j in range(BODY):
                        layer0_chunk(img, w, j)
                act.wait_ge(s["qf1"], after(img))
                nc.scalar.activation(qnorm[:, :], qnorm[:, :], ACT.Sqrt).then_inc(s["qn_ready"], 1)
                act.wait_ge(s["cleared"], after(img))
                f0 = img * IMG_CH
                features(f0, 0)
                silus(f0, 0)
                take_dbl(f0)
                softplus_start(f0)
                softplus_log(f0)
                body(f0, first=True)
                with act.Fori(1, BODIES - 1) as w:
                    body(img * IMG_CH + w * BODY)
                body(img * IMG_CH + (IMG_CH - BODY), last=True)

            act.wait_ge(s["mom1"], after(0))
            nc.scalar.activation(mom[:, 1:2], mom[:, 1:2], ACT.Sqrt).then_inc(s["std_ready"], 1)
            act.wait_ge(s["mom_ready"], after(0))
            with act.Fori(0, B) as img:
                with act.Fori(0, N // (2 * FIN)) as w:
                    for p in range(2):
                        it = img * (N // FIN) + w * 2 + p
                        act.wait_ge(fin_loaded[p], (img * (N // FIN // 2) + w) * 32 + 32)
                        nc.scalar.activation(fin_x[p], fin_x[p], ACT.Identity, bias=mom[:, 3:4],
                                             scale=mom[:, 2:3]).then_inc(s["fin_a"], 1)
                        act.wait_ge(s["fin_v"], after(it))
                        act.dma_start(out[bass.ds(img, 1), :, bass.ds((w * 2 + p) * FIN, FIN)]
                                      .rearrange("a c n -> (a c) n"), fin_y[p]).then_inc(out_stored[p], 16)

        @block.vector
        def _(dve):
            raise_credit(dve, "vector")
            nc.vector.memset(conv_mask[:, 0:DI], 0.0)
            nc.vector.memset(conv_mask[0:96, DI:2 * DI], 0.0)
            nc.vector.memset(conv_mask[96:128, DI:2 * DI], 1.0).then_inc(s["dve_setup"], 1)
            nc.vector.memset(ones[:, :], 1.0)
            nc.vector.memset(sums[:, :], 0.0)
            nc.vector.memset(kn[:, :, :, :], 1.0)
            nc.vector.memset(mv_t4[:, :, :], 0.0)
            nc.vector.memset(g_rep[:, :, :, :], 0.0)
            nc.vector.memset(g[:, :, :], 0.0)
            nc.vector.memset(w_edge[:, :], 0.0)
            nc.vector.memset(carry[:, :, :], 0.0).then_inc(s["dve_setup"], 1)
            dve.wait_ge(loaded, 16 * N_LOADS)
            dve.wait_ge(s["dve_setup"], after(1))
            nc.vector.tensor_scalar(A[:, :, :], A[:, :, :], LOG_MAX, None, ALU.min)
            nc.vector.tensor_scalar(bn_tmp[:, 0:1], bn_v, BN_EPS, None, ALU.add).then_inc(s["dve_setup"], 1)
            dve.wait_ge(s["act_setup"], after(1))
            nc.vector.reciprocal(bn_tmp[:, 1:2], bn_tmp[:, 1:2]).then_inc(s["mom2"], 1)
            dve.wait_ge(s["mom2"], after(0))
            nc.vector.tensor_tensor(bn_tmp[:, 2:3], bn_tmp[:, 1:2], bn_s, ALU.mult).then_inc(s["mom2"], 1)
            dve.wait_ge(s["mom2"], after(1))
            nc.vector.tensor_tensor(bn_tmp[:, 0:1], bn_tmp[:, 2:3], bn_m, ALU.mult).then_inc(s["mom2"], 1)
            dve.wait_ge(s["mom2"], after(2))
            nc.vector.tensor_tensor(bn_tmp[:, 3:4], bn_b, bn_tmp[:, 0:1], ALU.subtract)
            nc.vector.tensor_scalar(A[:, :, :], A[:, :, :], -1.0, None, ALU.mult).then_inc(s["dve_setup"], 1)

            def over_tiles(row, count):
                return row[:, None, :].broadcast_to([128, count, M])

            def layer0_chunk(img, w, j):
                q = img * IMG_CH + w * BODY + j
                for pair in range(2):
                    dve.wait_ge(s["xt_ready"], after(q * 2 + pair))
                    dve.wait_ge(s["kn_ready"], after(q - 1))
                    nc.vector.tensor_tensor(keys[:, 2 * pair:2 * pair + 2, :], xk_ps[pair][:, :, 128:],
                                            over_tiles(bk_b, 2), ALU.add).then_inc(s["k_taken"], 1)
                dve.wait_ge(s["k_taken"], after(q * 2 + 1))
                nc.vector.tensor_tensor(keys_sq[:, :, :], keys[:, :, :], keys[:, :, :], ALU.mult) \
                    .then_inc(s["k_sq"], 1)
                dve.wait_ge(s["k_sq"], after(q))
                dve.wait_ge(s["kn_ready"], after(q - 1))
                nc.vector.tensor_reduce(knorm[:, :], keys_sq[:, :, :], AX.X, ALU.add).then_inc(s["k_red"], 1)
                dve.wait_ge(s["rk_ready"], after(q))
                dve.wait_ge(s["s_done"], after(q - 2))
                nc.vector.tensor_tensor(kn[:, j % 2, :, 0:M], keys[:, :, :],
                                        knorm[:, :, None].broadcast_to([128, TILES, M]), ALU.mult) \
                    .then_inc(s["kn_ready"], 1)
                dve.wait_ge(s["s_done"], after(q))
                dve.wait_ge(s["s_taken"], after(q - 1))
                nc.vector.tensor_tensor(sums[:, :], sums[:, :], s_ps, ALU.add).then_inc(s["s_taken"], 1)
                dve.wait_ge(s["q_done"], after(q))
                nc.vector.tensor_tensor(q_raw[:, bass.ds((w * BODY + j) * TILES, TILES), :],
                                        q_ps.rearrange("p (a m) -> p a m", m=M), over_tiles(bq_b, TILES),
                                        ALU.add).then_inc(s["q_taken"], 1)

            def finish_image(img):
                q_last = img * IMG_CH + (IMG_CH - 1)
                dve.wait_ge(s["s_taken"], after(q_last))
                dve.wait_ge(s["q_taken"], after(q_last))
                nc.vector.tensor_scalar(ksum_b[:, :], sums[:, F:F + M], NORM_EPS, None, ALU.add) \
                    .then_inc(s["ksb_ready"], 1)
                nt = N // 128
                nc.vector.tensor_tensor(sq_tmp, q_raw[:, :, :], q_raw[:, :, :], ALU.mult).then_inc(s["k_done"], 1)
                dve.wait_ge(s["k_done"], after(img * 5))
                nc.vector.tensor_reduce(qnorm[:, :], sq_tmp, AX.X, ALU.add).then_inc(s["qf1"], 1)
                dve.wait_ge(s["qf1"], after(img))
                dve.wait_ge(s["ksb_ready"], after(img))
                nc.vector.tensor_tensor(sq_tmp, q_raw[:, :, :], over_tiles(ksum_b, nt), ALU.mult) \
                    .then_inc(s["k_done"], 1)
                dve.wait_ge(s["k_done"], after(img * 5 + 1))
                nc.vector.tensor_reduce(qk[:, :], sq_tmp, AX.X, ALU.add).then_inc(s["k_done"], 1)
                dve.wait_ge(s["mvt_done"], after(img))
                nc.vector.tensor_scalar(mv_t4[:, :, 0:F], fe[:, None, 0:F].broadcast_to([128, TAPS, F]),
                                        gamma[:, 0:1], None, ALU.mult).then_inc(s["mvt_ready"], 1)
                dve.wait_ge(s["mv_done"], after(img))
                nc.vector.tensor_scalar(mv_all[:, bass.ds(img, 1), :].rearrange("m a c -> m (a c)"),
                                        c_ps[0:F, 0:128], gamma[0:F, 0:1], None, ALU.mult).then_inc(s["mv_ready"], 1)
                dve.wait_ge(s["qn_ready"], after(img))
                dve.wait_ge(s["k_done"], after(img * 5 + 2))
                nc.vector.scalar_tensor_tensor(qk[:, :], qnorm[:, :], float(N), qk[:, :], ALU.mult, ALU.add) \
                    .then_inc(s["k_done"], 1)
                dve.wait_ge(s["k_done"], after(img * 5 + 3))
                nc.vector.reciprocal(qk[:, :], qk[:, :]).then_inc(s["k_done"], 1)
                dve.wait_ge(s["k_done"], after(img * 5 + 4))
                nc.vector.tensor_tensor(g_t[:, :, M:F], qnorm[:, :, None], qk[:, :, None], ALU.mult)
                nc.vector.tensor_tensor(g_t[:, :, 0:M], q_raw[:, :, :],
                                        qk[:, :, None].broadcast_to([128, nt, M]), ALU.mult).then_inc(s["gt_ready"], 1)
                dve.wait_ge(s["p4_done"], after(img))
                nc.vector.tensor_tensor(w_xz[:, :], ycur[0][:, :], conv_mask[:, :], ALU.mult).then_inc(s["w_ready"], 1)
                for k in range(4):
                    nc.vector.memset(by_state(decay[k])[:, :, 0:1], 0.0)
                dve.wait_ge(s["mv_done"], after(img))
                nc.vector.memset(sums[:, :], 0.0).then_inc(s["cleared"], 1)
                dve.wait_ge(s["cleared"], after(img))

            def features(f, local):
                dve.wait_ge(s["gt_done"], after(f - 1))
                nc.vector.tensor_copy(g_rep[:, :, :, 0:F],
                                      g_t[:, bass.ds(local * TILES, TILES), None, :].broadcast_to([128, TILES, TAPS, F])) \
                    .then_inc(s["g_rep_ready"], 1)

            def split(f, par):
                dve.wait_ge(s["dbl_ready"], after(f))
                dve.wait_ge(s["c_done"], after(f * S - S - 1))
                nc.vector.tensor_copy(parts[:, par, :], dbl[0:BC3, :]).then_inc(s["split1"], 1)
                dve.wait_ge(s["split1"], after(f))
                nc.vector.tensor_tensor(resid[:, :], dbl[0:64, :], parts[0:64, par, :], ALU.subtract) \
                    .then_inc(s["split2"], 1)
                dve.wait_ge(s["split2"], after(f))
                nc.vector.tensor_copy(parts[0:64, par, :], resid[:, :]).then_inc(s["split3"], 1)
                dve.wait_ge(s["split3"], after(f))
                nc.vector.tensor_tensor(resid[0:32, :], resid[0:32, :], parts[0:32, par, :], ALU.subtract) \
                    .then_inc(s["split4"], 1)
                dve.wait_ge(s["split4"], after(f))
                nc.vector.tensor_copy(parts[0:32, par, :], resid[0:32, :]).then_inc(s["parts_ready"], 1)

            def softplus_mid(f):
                dve.wait_ge(s["sp_exp"], after(f))
                dve.wait_ge(s["sp4"], after(f - 1))
                nc.vector.tensor_scalar(sp_w[:, :, :], sp_e[:, :, :], 1.0, None, ALU.add).then_inc(s["sp1"], 1)
                dve.wait_ge(s["sp1"], after(f))
                nc.vector.scalar_tensor_tensor(sp_c[:, :, :], sp_w[:, :, :], 1.0, sp_e[:, :, :],
                                               ALU.subtract, ALU.subtract).then_inc(s["sp2"], 1)

            def softplus_end(f, par):
                dve.wait_ge(s["sp_ln"], after(f))
                dve.wait_ge(s["sp2"], after(f))
                nc.vector.tensor_tensor(sp_c[:, :, :], sp_w[:, :, :], sp_c[:, :, :], ALU.subtract).then_inc(s["sp3"], 1)
                dve.wait_ge(s["sp3"], after(f))
                nc.vector.scalar_tensor_tensor(sp_c[:, :, :], sp_e[:, :, :], 0.5, sp_c[:, :, :],
                                               ALU.mult, ALU.max).then_inc(s["sp4"], 1)
                dve.wait_ge(s["sp4"], after(f))
                dve.wait_ge(s["sp_lin"], after(f * 2 + 1))
                dve.wait_ge(s["decay_ready"], after(f * UNITS - UNITS - 1))
                nc.vector.tensor_tensor(dt[:, par, :, :], sp_r[:, :, :], sp_c[:, :, :], ALU.add).then_inc(s["dt_ready"], 1)
                dve.wait_ge(s["dt_ready"], after(f))
                dve.wait_ge(s["xm_ready"], after(f * 2 + 1))
                nc.vector.tensor_tensor(u[:, par, :, :], dt[:, par, :, :], xm[:, par, :, :], ALU.mult) \
                    .then_inc(s["u_ready"], 1)

            def fill(q, grp, h, par):
                k = 2 * grp + h
                unit = by_state(state[2 * (grp % 2) + h])
                if h == 0:
                    dve.wait_ge(s["b_done"], after(q * GROUPS + grp))
                    dve.wait_ge(s["u_ready"], after(q))
                dve.wait_ge(s["summed"], after(q * UNITS + (k - 4)))
                fill = nc.vector.tensor_tensor(unit[:, :, 1:SEG], u[:, par, h, None, :].broadcast_to([128, GRP, CH]),
                                               b_ps[:, :, :], ALU.mult)
                if h == 1:
                    fill.then_inc(s["b_used"], 1)
                dve.wait_ge(s["carried"], after(q * UNITS + (k - UNITS)))
                nc.vector.tensor_copy(unit[:, :, 0:1], carry[:, k, :, None]).then_inc(s["filled"], 1)

            def scan(q, grp, h):
                k = 2 * grp + h
                slot = 2 * (grp % 2) + h
                dve.wait_ge(s["filled"], after(q * UNITS + k))
                dve.wait_ge(s["decay_ready"], after(q * UNITS + k))
                nc.vector.tensor_tensor_scan(state[slot], decay[slot], state[slot], 0.0, ALU.mult, ALU.add) \
                    .then_inc(s["scanned"], 1)

            def keep(q, grp, h):
                k = 2 * grp + h
                dve.wait_ge(s["scanned"], after(q * UNITS + k))
                nc.vector.tensor_copy(carry[:, k, :, None], by_state(state[2 * (grp % 2) + h])[:, :, SEG - 1:SEG]) \
                    .then_inc(s["carried"], 1)

            def gate(q, par):
                dve.wait_ge(s["summed"], after(q * UNITS + (UNITS - 1)))
                dve.wait_ge(s["outp_done"], after(q - 1))
                dve.wait_ge(s["z_ready"], after(q * 2 + 1))
                for h in range(HALVES):
                    nc.vector.scalar_tensor_tensor(yt[:, h, :], xm[:, par, h, :], Dp[:, h:h + 1], ycur[h][:, :],
                                                   ALU.mult, ALU.add).then_inc(s["y_taken"], 1)
                dve.wait_ge(s["y_taken"], after(q * 2 + 1))
                nc.vector.tensor_tensor(yt[:, :, :], yt[:, :, :], zs[:, par, :, :], ALU.mult).then_inc(s["gated"], 1)

            def channel_stats(q, par):
                dve.wait_ge(s["xr_ready"], after(q))
                nc.vector.bn_stats(stats[:, bass.ds(q, 1), :].rearrange("p a k -> p (a k)"), xr[:, par, :]) \
                    .then_inc(s["stat_done"], 1)

            def body(q0, l0, first=False, last=False):
                for j in range(BODY):
                    q, f = q0 + j, q0 + (j + 1)
                    prev, ahead = not (first and j == 0), not (last and j == BODY - 1)
                    for grp in range(GROUPS):
                        fill(q, grp, 0, j % 2)
                        if grp == 0 and ahead:
                            features(f, l0 + (j + 1))
                        scan(q, grp, 0)
                        if grp == 3 and ahead:
                            softplus_end(f, (j + 1) % 2)
                        fill(q, grp, 1, j % 2)
                        keep(q, grp, 0)
                        scan(q, grp, 1)
                        if grp == 0 and prev:
                            gate(q - 1, (j - 1) % 2)
                        if grp == 2 and ahead:
                            split(f, (j + 1) % 2)
                            softplus_mid(f)
                        if grp == 3 and prev:
                            channel_stats(q - 1, (j - 1) % 2)
                        keep(q, grp, 1)
                if last:
                    gate(q0 + (BODY - 1), (BODY - 1) % 2)
                    channel_stats(q0 + (BODY - 1), (BODY - 1) % 2)

            with dve.Fori(0, B) as img:
                with dve.Fori(0, BODIES) as w:
                    for j in range(BODY):
                        layer0_chunk(img, w, j)
                finish_image(img)
                f0 = img * IMG_CH
                dve.wait_ge(s["gt_ready"], after(img))
                features(f0, 0)
                split(f0, 0)
                softplus_mid(f0)
                softplus_end(f0, 0)
                dve.wait_ge(s["xz_done"], after(f0 * 4 + 3))
                nc.vector.tensor_copy(w_edge[:, :], w_xz[:, 0:DI]).then_inc(s["edge_ready"], 1)
                body(f0, 0, first=True)
                with dve.Fori(1, BODIES - 1) as w:
                    body(img * IMG_CH + w * BODY, w * BODY)
                body(img * IMG_CH + (IMG_CH - BODY), IMG_CH - BODY, last=True)

            dve.wait_ge(s["stat_done"], after(CHUNKS - 1))
            nc.vector.bn_aggr(mom[:, 0:2], stats[:, :, :].rearrange("p a k -> p (a k)")).then_inc(s["mom2"], 1)
            dve.wait_ge(s["mom2"], after(3))
            nc.vector.tensor_scalar(mom[:, 1:2], mom[:, 1:2], BN_EPS, None, ALU.add).then_inc(s["mom1"], 1)
            dve.wait_ge(s["std_ready"], after(0))
            nc.vector.reciprocal(mom[:, 1:2], mom[:, 1:2]).then_inc(s["mom2"], 1)
            dve.wait_ge(s["mom2"], after(4))
            nc.vector.tensor_tensor(mom[:, 2:3], mom[:, 1:2], bn2[:, 0:1], ALU.mult).then_inc(s["mom2"], 1)
            dve.wait_ge(s["mom2"], after(5))
            nc.vector.tensor_tensor(mom[:, 0:1], mom[:, 0:1], mom[:, 2:3], ALU.mult).then_inc(s["mom2"], 1)
            dve.wait_ge(s["mom2"], after(6))
            nc.vector.tensor_tensor(mom[:, 3:4], bn2[:, 1:2], mom[:, 0:1], ALU.subtract).then_inc(s["mom_ready"], 1)
            with dve.Fori(0, B) as img:
                dve.wait_ge(s["fin_mm"], after(img * (N // FIN) - 1))
                nc.vector.tensor_copy(mv_now[:, :], mv_all[:, bass.ds(img, 1), :].rearrange("m a c -> m (a c)")) \
                    .then_inc(s["mvnow_ready"], 1)
                with dve.Fori(0, N // (2 * FIN)) as w:
                    for p in range(2):
                        it = img * (N // FIN) + w * 2 + p
                        dve.wait_ge(s["fin_a"], after(it))
                        dve.wait_ge(out_stored[p], (img * (N // FIN // 2) + w) * 16 + 16)
                        nc.vector.scalar_tensor_tensor(fin_y[p], fin_x[p], 0.2, fin_x[p], ALU.mult, ALU.max) \
                            .then_inc(s["fin_done"], 1)
                        dve.wait_ge(s["fin_done"], after(it))
                        dve.wait_ge(s["fin_mm"], after(it))
                        nc.vector.tensor_tensor(fin_y[p], fin_y[p], b_ps[:, :, :].rearrange("p a n -> p (a n)"),
                                                ALU.add).then_inc(s["fin_v"], 1)

        @block.gpsimd
        def _(pool):
            raise_credit(pool, "gpsimd")

            def body(q0):
                for j in range(BODY):
                    for k in range(UNITS):
                        grp, h = k // 2, k % 2
                        unit = by_state(state[2 * (grp % 2) + h])
                        pool.wait_ge(s["carried"], after((q0 + j) * UNITS + k))
                        if h == 0:
                            pool.wait_ge(s["c_ready"], after((q0 + j) * S + (GRP * grp + GRP - 1)))
                        nc.gpsimd.tensor_tensor(unit[:, :, 1:SEG], unit[:, :, 1:SEG], c_sb[:, grp % 2, :, :],
                                                ALU.mult).then_inc(s["weighted"], 1)

            with pool.Fori(0, B) as img:
                with pool.Fori(0, BODIES) as w:
                    body(img * IMG_CH + w * BODY)


N_LOADS = 30


def kernel(**inputs):
    import numpy as np
    import ml_dtypes
    import concourse.bacc as bacc
    from concourse import mybir
    from concourse.bass_utils import run_bass_kernel_spmd

    a = {k.replace("L0_conv_", "").replace("L1_conv_", "m_"): np.asarray(v) for k, v in inputs.items()}
    x = np.zeros((B, C, HP, WP), np.float32)
    x[:, :, PAD:PAD + H, PAD:PAD + W] = a["x"]
    taps = [a[f"w{b}"].reshape(32, 128, 9).transpose(1, 2, 0) for b in (2, 3, 4)]
    onehot = np.zeros((3, 2 * S, 2 * S, 128), ml_dtypes.bfloat16)
    for n in range(2 * S):
        onehot[:, n, n, :] = 1
    xp = a["m_x_proj_w"]
    bc = xp[RANK:].T
    halves = lambda v: np.ascontiguousarray(v.reshape(HALVES, 128).T)
    arrays = {
        "x": x, "ident": np.eye(128, dtype=np.float32), "onehot": onehot.reshape(BC3, 2 * S, 128),
        "w_taps": np.concatenate(taps, 1),
        "w_mid": np.concatenate([a["w1"].reshape(32, 128).T] + [p[:, 4] for p in taps], 1),
        "bn_scale": a["bn_scale"].reshape(128, 1), "bn_bias": a["bn_bias"].reshape(128, 1),
        "bn_mean": a["bn_mean"].reshape(128, 1), "bn_var": a["bn_var"].reshape(128, 1),
        "wq": a["wq"].reshape(M, 128).T, "wk": a["wk"].reshape(M, 128).T, "wv": a["wv"].reshape(128, 128).T,
        "bq": a["bq"].reshape(1, M), "bk": a["bk"].reshape(1, M), "bv": a["bv"].reshape(1, 128),
        "gamma": a["gamma"].reshape(1, 1), "w_in": a["m_in_proj_w"].T, "conv_w": a["m_conv_w"].T,
        "conv_b": halves(a["m_conv_b"]),
        "x_proj": np.concatenate([bc, bc, bc, xp[:RANK].T], 1).reshape(HALVES, 128, BC3 + RANK).transpose(1, 0, 2),
        "dt_w": a["m_dt_proj_w"].T, "dt_b": halves(a["m_dt_proj_b"]),
        "A_log": a["m_A_log"].reshape(HALVES, 128, S).transpose(1, 0, 2), "D": halves(a["m_D"]),
        "w_out": a["m_out_proj_w"].T.reshape(HALVES, 128, 128).transpose(1, 0, 2),
        "bn_gamma": a["m_bn_gamma"].reshape(128, 1), "bn_beta": a["m_bn_beta"].reshape(128, 1),
    }
    nc = bacc.Bacc("TRN2", target_bir_lowering=False, num_devices=1)
    feeds, t = {}, {}
    for name, v in arrays.items():
        v = np.ascontiguousarray(v)
        feeds[f"in_{name}"] = v
        t[name] = nc.dram_tensor(f"in_{name}", v.shape, mybir.dt.from_np(v.dtype), kind="ExternalInput").ap()
    out = nc.dram_tensor("out", (B, C, N), mybir.dt.float32, kind="ExternalOutput").ap()
    program(nc, t, out)
    r = run_bass_kernel_spmd(nc, [feeds], core_ids=[0])
    return r.results[0]["out"].reshape(B, C, H, W)
```

```python
import numpy as np
import concourse.bass as bass
from concourse import mybir
from contextlib import ExitStack

B, C, H, W = 8, 128, 128, 128
N = H * W
PAD = 18
HP = H + 2 * PAD
M = 16
F = M + 1
TAPS = 4
DI = 256
HALVES = DI // 128
S = 16
RANK = 8
CH = 512
ROWS = CH // W
TILES = CH // 128
WIN_CH = 2
WIN_ROWS = WIN_CH * ROWS + 2 * PAD
BODY = 4
IMG_CH = N // CH
BODIES = IMG_CH // BODY
CHUNKS = B * IMG_CH
PAIR = 2
UNITS = S // PAIR
ROWS_U = HALVES * PAIR
SEG = CH + 1
ADDED = (0, 1, 2, 3, 5, 6)
LAG = 2
TAPS_BY = (0, 4, 10, 15, 18, 21, 24, 25, 25)
BN_EPS, NORM_EPS = 1e-5, 1e-6
LOG_MAX = 82.9
FIN = 2048
FIN_BUFS = 4
FIN_TURNS = N // (FIN_BUFS * FIN)
BC3 = 3 * 2 * S
DIL = (6, 12, 18)
CREDIT = 32


def after(item):
    return item + 1 + CREDIT


def program(nc, t, out):
    f32, bf16 = mybir.dt.float32, mybir.dt.bfloat16
    ALU, ACT, AX = mybir.AluOpType, mybir.ActivationFunctionType, mybir.AxisListType
    ctx = ExitStack()
    with ctx:
        def sb(name, shape, dt=f32):
            return ctx.enter_context(nc.sbuf_tensor(name, shape, dt))

        def sem(name):
            return ctx.enter_context(nc.semaphore(name))

        xr_scr = nc.dram_tensor("xr_scr", (128, CHUNKS * CH), f32).ap()
        g_scr = nc.dram_tensor("g_scr", (F, CHUNKS * CH), f32).ap()
        g_tiles = nc.dram_tensor("g_tiles", (128, N // 128 * F), f32).ap()
        mv_scr = nc.dram_tensor("mv_scr", (F, B * 128), f32).ap()

        ident = sb("ident", [128, 128])
        ones = sb("ones", [128, 128])
        onehot = sb("onehot", [BC3, 2 * S, 128], bf16)
        w_taps = sb("w_taps", [128, 27, 32])
        w_mid = sb("w_mid", [128, 128])
        bn4 = sb("bn4", [128, 4])
        bn_s, bn_b, bn_m, bn_v = (bn4[:, k:k + 1] for k in range(4))
        bn_tmp = sb("bn_tmp", [128, 4])
        wq = sb("wq", [128, M])
        xk_rhs = sb("xk_rhs", [128, 128 + M])
        bq_b = sb("bq_b", [128, M])
        bk_b = sb("bk_b", [128, M])
        wv = sb("wv", [128, 128])
        bv = sb("bv", [1, 128])
        gamma = sb("gamma", [128, 1])
        w_in = sb("w_in", [128, 2 * DI])
        conv_mask = sb("conv_mask", [128, 2 * DI])
        conv_b = sb("conv_b", [128, HALVES])
        x_proj = sb("x_proj", [128, HALVES, BC3 + RANK])
        dt_w = sb("dt_w", [128, DI])
        dt_b = sb("dt_b", [128, HALVES])
        A = sb("A", [128, HALVES, S])
        Dp = sb("Dp", [128, HALVES])
        w_out = sb("w_out", [128, HALVES, 128])
        bn2 = sb("bn2", [128, 2])

        windows_mem = sb("windows_mem", [128, 2 * WIN_ROWS * W])
        xw = [windows_mem[:, p * WIN_ROWS * W:(p + 1) * WIN_ROWS * W].rearrange("c (r w) -> c r w", w=W)
              for p in range(2)]
        units_mem = sb("units_mem", [128, 6 * ROWS_U * SEG])
        slots = [units_mem[:, k * ROWS_U * SEG:(k + 1) * ROWS_U * SEG] for k in range(6)]
        state, decay = slots[0:4], slots[4:6]

        def stretches(unit):
            return unit.rearrange("c (h n t) -> c h n t", h=HALVES, n=PAIR)

        y_relu = sb("y_relu", [128, CH])
        x_t = sb("x_t", [128, TILES, 128])
        keys = sb("keys", [128, TILES, M])
        keys_sq = sb("keys_sq", [128, TILES, M])
        knorm = sb("knorm", [128, TILES])
        kn = sb("kn", [128, TILES, F])
        q_feat = sb("q_feat", [128, N // 128, F])
        sums = sb("sums", [128, 2 * F])
        ksum_b = sb("ksum_b", [128, M])
        qk = sb("qk", [128, N // 128])
        mv_t4 = sb("mv_t4", [128, TAPS, 32])
        mv_now = sb("mv_now", [F, 128])
        w_xz = sb("w_xz", [128, 2 * DI])
        w_edge = sb("w_edge", [128, DI])

        g_tile = sb("g_tile", [128, 2, TILES, F])
        g_rep = sb("g_rep", [128, TILES, TAPS, 32])
        g = sb("g", [128, 2, CH + TAPS - 1])
        xm = sb("xm", [128, 2, HALVES, CH])
        zs = sb("zs", [128, HALVES, CH])
        dbl = sb("dbl", [BC3 + RANK, CH])
        resid = sb("resid", [64, CH])
        parts = sb("parts", [BC3, 2, CH], bf16)
        sp = sb("sp", [128, 4, HALVES, CH])
        sp_e, sp_w, sp_c, sp_r = (sp[:, k, :, :] for k in range(4))
        yt = sp_r
        sq_tmp = sp[:, 0:2, :, :].rearrange("p k h t -> p (k h t)").rearrange("p (a m) -> p a m", m=M)
        dt = sb("dt", [128, HALVES, CH])
        u = sb("u", [128, 2, HALVES, CH])
        c_sb = sb("c_sb", [128, 2, PAIR, CH])
        carry = sb("carry", [128, UNITS, ROWS_U])
        xr = sb("xr", [128, CH])
        stats = sb("stats", [128, CHUNKS, 6])
        mom = sb("mom", [128, 4])

        fin_x = [units_mem[:, k * FIN:(k + 1) * FIN] for k in range(FIN_BUFS)]
        fin_y = [units_mem[:, k * FIN:(k + 1) * FIN] for k in (FIN_BUFS, FIN_BUFS + 1)]
        fin_g = [windows_mem[0:F, B * 128 + k * FIN:B * 128 + (k + 1) * FIN] for k in range(FIN_BUFS)]
        mv_all = windows_mem[0:F, 0:B * 128].rearrange("m (b c) -> m b c", c=128)

        banks = ctx.enter_context(nc.psum_tensor("banks", [128, 8, CH], f32))
        b_ps = [banks[:, k, :] for k in (0, 1)]
        c_ps = banks[:, 2, :]
        y_ps = [banks[:, k, :] for k in (3, 4)]
        fe = banks[:, 5, :]
        xz_ps = [c_ps, fe]
        conv_ps = banks[:, 6, :]
        xk_ps = banks[:, 7, 0:2 * (128 + M)].rearrange("p (a n) -> p a n", a=2)
        s_ps = banks[:, 7, 288:288 + 2 * F]
        q_ps = banks[:, 7, 352:352 + TILES * M]
        mvt_ps = banks[:, 7, 0:F]
        mv_ps = banks[0:F, 7, 64:192]
        fin_ps = [banks[:, 0:4, :], banks[:, 4:8, :]]

        loaded = sem("loaded")
        win_loaded = [sem(f"win_loaded{p}") for p in range(2)]
        tile_loaded = [sem(f"tile_loaded{p}") for p in range(2)]
        feat_stored = [sem(f"feat_stored{p}") for p in range(2)]
        xr_stored, image_stored, mv_loaded = sem("xr_stored"), sem("image_stored"), sem("mv_loaded")
        fin_loaded = [sem(f"fin_loaded{p}") for p in range(FIN_BUFS)]
        out_stored = [sem(f"out_stored{p}") for p in range(2)]
        counting = {}
        for who, names in {
            "tensor": "conv_done xk_done s_done q_done mvt_done mv_done p4_done gt_done x_done z_done dbl_done "
                      "dtm_done b_done c_done summed outp_done fin_mm".split(),
            "vector": "dve_setup k_taken k_sq k_red kn_ready q_taken s_taken q_steps ksb_ready q_norm2 g_ready cleared "
                      "mvt_ready mv_ready w_ready g_rep_ready split2 split3 split4 parts_ready sp2 sp3 sp4 "
                      "dt_ready u_ready b_used filled scanned carried y_taken gated stat_done edge_ready mom1 mom2 "
                      "mom_ready fin_v fin_done mvnow_ready".split(),
            "scalar": "act_setup relu_done xt_ready lnk rk_ready qn_ready g_copied x_ready z_ready split1 dbl_ready "
                      "sp_lin sp_abs sp_exp sp1 sp_ln decay_ready c_ready xr_ready std_ready fin_a".split(),
            "gpsimd": "multiplied weighted".split(),
        }.items():
            for name in names:
                counting[name] = sem(name)
                counting.setdefault(who, []).append(counting[name])
        s = counting

        block = ctx.enter_context(nc.Block())

        def raise_credit(e, who):
            for x in s[who]:
                e.sem_inc(x, CREDIT)

        @block.sync
        def _(sync):
            for x in (*feat_stored, xr_stored, image_stored, *out_stored):
                sync.sem_inc(x, 16)
            bn = [(bn4[:, k:k + 1], t[n]) for k, n in enumerate(("bn_scale", "bn_bias", "bn_mean", "bn_var"))]
            loads = bn + [
                (ident[:, :], t["ident"]), (onehot[:, :, :], t["onehot"]), (w_taps[:, :, :], t["w_taps"]),
                (w_mid[:, :], t["w_mid"]), (wq[:, :], t["wq"]), (xk_rhs[:, 0:128], t["ident"]),
                (xk_rhs[:, 128:], t["wk"]), (bq_b[:, :], t["bq"].broadcast_to([128, M])),
                (bk_b[:, :], t["bk"].broadcast_to([128, M])), (wv[:, :], t["wv"]), (bv[:, :], t["bv"]),
                (gamma[:, :], t["gamma"].broadcast_to([128, 1])), (w_in[:, :], t["w_in"]),
                (conv_b[:, :], t["conv_b"]), (x_proj[:, :, :], t["x_proj"]), (dt_w[BC3:BC3 + RANK, :], t["dt_w"]),
                (dt_b[:, :], t["dt_b"]), (A[:, :, :], t["A_log"]), (Dp[:, :], t["D"]),
                (w_out[:, :, :], t["w_out"]), (bn2[:, 0:1], t["bn_gamma"]), (bn2[:, 1:2], t["bn_beta"]),
            ]
            sync.wait_ge(s["dve_setup"], after(0))
            loads += [(conv_mask[32 * k:32 * k + F, 0:DI], t["conv_w"][k:k + 1, :].broadcast_to([F, DI]))
                      for k in range(TAPS)]
            assert len(loads) == N_LOADS
            for dst, src in loads:
                sync.dma_start(dst, src).then_inc(loaded, 16)

            def window(img, w, p, c_free):
                sync.wait_ge(s["conv_done"], after(c_free))
                row = w * (BODY * ROWS) + p * WIN_CH * ROWS
                sync.dma_start(xw[p], t["x"][bass.ds(img, 1), :, bass.ds(row, WIN_ROWS), :]
                               .rearrange("a c r w -> (a c) r w")).then_inc(win_loaded[p], 16)

            def first_windows(img):
                for p in range(2):
                    window(img, 0, p, img * IMG_CH - WIN_CH * (2 - p) + WIN_CH - 1)

            def load_tile(f, local, par):
                sync.wait_ge(s["g_rep_ready"], after(f - 2))
                sync.dma_start(g_tile[:, par, :, :].rearrange("p a m -> p (a m)"),
                               g_tiles[:, bass.ds(local * TILES * F, TILES * F)]).then_inc(tile_loaded[par], 16)

            def store_features(f, par):
                sync.wait_ge(s["g_copied"], after(f))
                sync.dma_start(g_scr[:, bass.ds(f * CH, CH)], g[96:96 + F, par, 0:CH]).then_inc(feat_stored[par], 16)

            def store_xr(q):
                sync.wait_ge(s["xr_ready"], after(q))
                sync.dma_start(xr_scr[:, bass.ds(q * CH, CH)], xr[:, :]).then_inc(xr_stored, 16)

            def store_image(img):
                sync.wait_ge(s["g_ready"], after(img))
                sync.wait_ge(s["g_rep_ready"], after(img * IMG_CH - 1))
                sync.dma_start(g_tiles[:, :], q_feat[:, :, :].rearrange("p a m -> p (a m)")).then_inc(image_stored, 16)
                sync.wait_ge(s["mv_ready"], after(img))
                sync.dma_start(mv_scr[:, bass.ds(img * 128, 128)], mv_now[:, :]).then_inc(image_stored, 16)
                sync.wait_ge(image_stored, img * 32 + 48)

            def body(img, w, layer0, first=False, last=False):
                for j in range(BODY):
                    q = img * IMG_CH + w * BODY + j
                    ahead = not (last and j == BODY - 1)
                    if ahead:
                        load_tile(q + 1, w * BODY + (j + 1), (j + 1) % 2)
                        store_features(q + 1, (j + 1) % 2)
                    if not (first and j == 0):
                        store_xr(q - 1)
                    if layer0 and j % 2 and not last:
                        window(img + 1, w + 1, j // 2, q + IMG_CH)

            def section(img, layer0):
                if layer0:
                    first_windows(img + 1)
                load_tile(img * IMG_CH, 0, 0)
                store_features(img * IMG_CH, 0)
                body(img, 0, layer0, first=True)
                with sync.Fori(1, BODIES - 1) as w:
                    body(img, w, layer0)
                body(img, BODIES - 1, layer0, last=True)

            first_windows(0)
            with sync.Fori(0, BODIES - 1) as w:
                for p in range(2):
                    window(0, w + 1, p, w * BODY + 2 * p + 1)
            store_image(0)
            with sync.Fori(0, B - 1) as img:
                section(img, True)
                store_image(img + 1)
                store_xr(img * IMG_CH + (IMG_CH - 1))
            section(B - 1, False)
            store_xr(CHUNKS - 1)

            sync.wait_ge(xr_stored, 16 + 16 * CHUNKS)
            for p in range(2):
                sync.wait_ge(feat_stored[p], 16 + 16 * (CHUNKS // 2))
            sync.dma_start(mv_all, mv_scr.rearrange("m (b c) -> m b c", c=128)).then_inc(mv_loaded, 16)
            with sync.Fori(0, B) as img:
                with sync.Fori(0, FIN_TURNS) as w:
                    for p in range(FIN_BUFS):
                        it = img * (N // FIN) + w * FIN_BUFS + p
                        sync.wait_ge(s["fin_done"], after(it - FIN_BUFS))
                        sync.wait_ge(s["fin_mm"], after(it - FIN_BUFS))
                        sync.dma_start(fin_x[p], xr_scr[:, bass.ds(it * FIN, FIN)]).then_inc(fin_loaded[p], 16)
                        sync.dma_start(fin_g[p], g_scr[:, bass.ds(it * FIN, FIN)]).then_inc(fin_loaded[p], 16)
            for p in range(2):
                sync.wait_ge(out_stored[p], 16 + 16 * (B * N // FIN // 2))

        @block.tensor
        def _(pe):
            raise_credit(pe, "tensor")
            pe.wait_ge(loaded, 16 * N_LOADS)
            pe.wait_ge(s["dve_setup"], after(1))

            def keys_and_xt(c, lb, j, pair):
                p, r0 = j // WIN_CH, PAD + (j % WIN_CH) * ROWS + 2 * pair
                if pair == 0:
                    if j % WIN_CH == 0:
                        pe.wait_ge(win_loaded[p], lb * 16 + 16)
                    pe.wait_ge(s["q_taken"], after(c - 1))
                else:
                    pe.wait_ge(s["k_taken"], after(c * 2))
                for a in range(2):
                    tile = nc.tensor.matmul(xk_ps[:, a, :], xw[p][:, r0 + a, :], xk_rhs[:, :], start=True, stop=True)
                tile.then_inc(s["xk_done"], 1)

            taps = [(4, None)] + [(k, b) for k in range(9) if k != 4 for b in range(3)]

            def convolve(c, j, k0, k1):
                p, r0 = j // WIN_CH, PAD + (j % WIN_CH) * ROWS
                for n in range(k0, k1):
                    k, b = taps[n]
                    if b is None:
                        pe.wait_ge(s["relu_done"], after(c - 1))
                        tap = nc.tensor.matmul(conv_ps, w_mid[:, :], xw[p][:, r0:r0 + ROWS, :], start=True, stop=True)
                        continue
                    dy, dx = (k // 3 - 1) * DIL[b], (k % 3 - 1) * DIL[b]
                    lo, hi = max(0, -dx), W - max(0, dx)
                    dst = conv_ps[32 * b + 32:32 * b + 64, :].rearrange("o (r w) -> o r w", w=W)
                    tap = nc.tensor.matmul(dst[:, :, lo:hi], w_taps[:, 9 * b + k, :],
                                           xw[p][:, r0 + dy:r0 + dy + ROWS, lo + dx:hi + dx], start=False,
                                           stop=True, skip_group_check=True)
                if k1 == len(taps) and k0 < k1:
                    tap.then_inc(s["conv_done"], 1)

            def key_sums(c):
                pe.wait_ge(s["kn_ready"], after(c))
                for a in range(TILES):
                    nc.tensor.matmul(s_ps[:, 0:F], x_t[:, a, :], kn[:, a, :], start=a == 0, stop=a == TILES - 1)
                for a in range(TILES):
                    tile = nc.tensor.matmul(s_ps[:, F:2 * F], ones[:, :], kn[:, a, :],
                                            start=a == 0, stop=a == TILES - 1)
                tile.then_inc(s["s_done"], 1)

            def queries(c):
                pe.wait_ge(s["relu_done"], after(c))
                pe.wait_ge(s["s_taken"], after(c))
                for a in range(TILES):
                    tile = nc.tensor.matmul(q_ps[:, a * M:(a + 1) * M], y_relu[:, a * 128:(a + 1) * 128],
                                            wq[:, :], start=True, stop=True)
                tile.then_inc(s["q_done"], 1)

            def image_weights(img):
                pe.wait_ge(s["ksb_ready"], after(img))
                nc.tensor.matmul(mvt_ps, wv[:, :], sums[:, 0:F], start=True, stop=False)
                nc.tensor.matmul(mvt_ps, bv[0:1, :], sums[0:1, F:2 * F], start=False, stop=True) \
                    .then_inc(s["mvt_done"], 1)
                pe.wait_ge(s["mvt_ready"], after(img))
                nc.tensor.matmul(mv_ps, sums[:, 0:F], wv[:, :], start=True, stop=False)
                nc.tensor.matmul(mv_ps, sums[0:1, F:2 * F], bv[0:1, :], start=False, stop=True) \
                    .then_inc(s["mv_done"], 1)
                nc.tensor.matmul(conv_ps, mv_t4[:, :, :].rearrange("p k m -> p (k m)"), w_in[:, :],
                                 start=True, stop=True).then_inc(s["p4_done"], 1)

            def features(f):
                pe.wait_ge(s["g_rep_ready"], after(f))
                for a in range(TILES):
                    tile = nc.tensor.matmul(fe[:, a * 128:(a + 1) * 128],
                                            g_rep[:, a, :, :].rearrange("p k m -> p (k m)"), ident[:, :],
                                            start=True, stop=True)
                tile.then_inc(s["gt_done"], 1)

            def project_x(f, par, h):
                nc.tensor.matmul(xz_ps[h], w_xz[:, h * 128:(h + 1) * 128], g[:, par, 0:CH], start=True, stop=True)
                nc.tensor.matmul(xz_ps[h][:, 0:TAPS - 1], w_edge[:, h * 128:(h + 1) * 128],
                                 g[:, 1 - par, CH:CH + TAPS - 1], start=False, stop=True,
                                 skip_group_check=True).then_inc(s["x_done"], 1)

            def project_z(q, par, h):
                nc.tensor.matmul(xz_ps[h], w_xz[:, DI + h * 128:DI + (h + 1) * 128], g[:, par, 0:CH],
                                 start=True, stop=True).then_inc(s["z_done"], 1)

            def project_dbl(f, par):
                for h in range(HALVES):
                    last = nc.tensor.matmul(fe[0:BC3 + RANK, :], x_proj[:, h, :], xm[:, par, h, :],
                                            start=h == 0, stop=h == 1)
                last.then_inc(s["dbl_done"], 1)

            def project_dt(f, h):
                pe.wait_ge(s["sp_lin" if h else "dbl_ready"], after(f * 2 if h else f))
                nc.tensor.matmul(fe, dt_w[BC3:BC3 + RANK, h * 128:(h + 1) * 128], dbl[BC3:BC3 + RANK, :],
                                 start=True, stop=True).then_inc(s["dtm_done"], 1)

            def spread_b(q, k, par):
                pe.wait_ge(s["parts_ready"], after(q))
                for i in range(PAIR):
                    pe.wait_ge(s["b_used"], after(q * S + (PAIR * k + i - 2)))
                    nc.tensor.matmul(b_ps[i], onehot[:, PAIR * k + i, :], parts[:, par, :],
                                     start=True, stop=True).then_inc(s["b_done"], 1)

            def spread_c(q, k, i, par):
                pe.wait_ge(s["c_ready"], after(q * S + (PAIR * k + i - 1)))
                nc.tensor.matmul(c_ps, onehot[:, S + PAIR * k + i, :], parts[:, par, :],
                                 start=True, stop=True).then_inc(s["c_done"], 1)

            def sum_unit(q, k):
                if k in ADDED:
                    pe.wait_ge(s["weighted"], after(q * len(ADDED) + ADDED.index(k)))
                else:
                    pe.wait_ge(s["multiplied"], after(q * UNITS + k))
                if k == 0:
                    pe.wait_ge(s["y_taken"], after(q * 2 - 1))
                terms = 1 if k in ADDED else PAIR
                for h in range(HALVES):
                    for i in range(terms):
                        last = nc.tensor.matmul(y_ps[h], ident[:, :], stretches(state[k % 4])[:, h, i, 1:SEG],
                                                start=k == 0 and i == 0, stop=k == UNITS - 1 and i == terms - 1)
                last.then_inc(s["summed"], 1)

            def project_out(q):
                pe.wait_ge(s["gated"], after(q))
                for h in range(HALVES):
                    last = nc.tensor.matmul(fe, w_out[:, h, :], yt[:, h, :], start=h == 0, stop=h == 1)
                last.then_inc(s["outp_done"], 1)

            def body(img, w, layer0, first=False, last=False):
                for j in range(BODY):
                    q = img * IMG_CH + w * BODY + j
                    f, c, lb, par = q + 1, q + IMG_CH, (img + 1) * BODIES + w, j % 2
                    prev, ahead = not (first and j == 0), not (last and j == BODY - 1)
                    for k in range(UNITS):
                        if k == 4:
                            pe.wait_ge(s["z_ready"], after(q * 2))
                        spread_c(q, k, 0, par)
                        if layer0 and k in (0, 2):
                            keys_and_xt(c, lb, j, k // 2)
                        if layer0 and k == 5:
                            key_sums(c)
                        if layer0:
                            convolve(c, j, TAPS_BY[k], TAPS_BY[k + 1])
                        if k == UNITS - 1:
                            if ahead:
                                spread_b(f, 0, 1 - par)
                        elif k != 4:
                            spread_b(q, k + 1, par)
                        if k == 4:
                            pe.wait_ge(s["z_ready"], after(q * 2 + 1))
                            if ahead:
                                project_dbl(f, 1 - par)
                        if k == 5 and ahead:
                            project_dt(f, 1)
                        spread_c(q, k, 1, par)
                        if k >= LAG:
                            sum_unit(q, k - LAG)
                        elif prev:
                            sum_unit(q - 1, UNITS - LAG + k)
                        if k == 1 and ahead:
                            features(f)
                        if k == 3:
                            if prev:
                                project_out(q - 1)
                            pe.wait_ge(s["c_ready"], after(q * S + (PAIR * k + 1)))
                            if ahead:
                                pe.wait_ge(s["g_copied"], after(f))
                                project_x(f, 1 - par, 0)
                            if prev:
                                pe.wait_ge(s["xr_ready"], after(q - 1))
                            if ahead:
                                project_x(f, 1 - par, 1)
                            spread_b(q, 5, par)
                            if ahead:
                                pe.wait_ge(s["x_ready"], after(f * 2))
                            project_z(q, par, 0)
                            if ahead:
                                pe.wait_ge(s["x_ready"], after(f * 2 + 1))
                            project_z(q, par, 1)
                        if k == 4 and ahead:
                            project_dt(f, 0)
                        if k == 6 and ahead:
                            pe.wait_ge(s["sp_lin"], after(f * 2 + 1))
                        if layer0 and k == UNITS - 1:
                            queries(c)

            def section(img, layer0):
                f0 = img * IMG_CH
                pe.wait_ge(s["w_ready"], after(img))
                features(f0)
                pe.wait_ge(s["c_ready"], after(f0 * S - 1))
                pe.wait_ge(s["g_copied"], after(f0))
                for h in range(HALVES):
                    project_x(f0, 0, h)
                pe.wait_ge(s["x_ready"], after(f0 * 2 + 1))
                project_dbl(f0, 0)
                for h in range(HALVES):
                    project_dt(f0, h)
                pe.wait_ge(s["sp_lin"], after(f0 * 2 + 1))
                pe.wait_ge(s["edge_ready"], after(img))
                spread_b(f0, 0, 0)
                body(img, 0, layer0, first=True)
                with pe.Fori(1, BODIES - 1) as w:
                    body(img, w, layer0)
                body(img, BODIES - 1, layer0, last=True)

            def flush(img):
                q = img * IMG_CH + (IMG_CH - 1)
                for k in range(UNITS - LAG, UNITS):
                    sum_unit(q, k)
                project_out(q)
                pe.wait_ge(s["xr_ready"], after(q))

            with pe.Fori(0, BODIES) as w:
                for j in range(BODY):
                    c = w * BODY + j
                    keys_and_xt(c, w, j, 0)
                    convolve(c, j, 0, 10)
                    keys_and_xt(c, w, j, 1)
                    convolve(c, j, 10, len(taps))
                    key_sums(c)
                    queries(c)
            image_weights(0)
            with pe.Fori(0, B - 1) as img:
                section(img, True)
                image_weights(img + 1)
                flush(img)
            section(B - 1, False)
            flush(B - 1)

            with pe.Fori(0, B) as img:
                with pe.Fori(0, FIN_TURNS) as w:
                    pe.wait_ge(s["mvnow_ready"], after(img))
                    for p in range(FIN_BUFS):
                        it = img * (N // FIN) + w * FIN_BUFS + p
                        pe.wait_ge(fin_loaded[p], (img * FIN_TURNS + w) * 32 + 32)
                        pe.wait_ge(s["fin_v"], after(it - 2))
                        for i in range(FIN // CH):
                            last = nc.tensor.matmul(fin_ps[p % 2][:, i, :], mv_now[:, :], fin_g[p][:, i * CH:(i + 1) * CH],
                                                    start=True, stop=True)
                        last.then_inc(s["fin_mm"], 1)

        @block.scalar
        def _(act):
            raise_credit(act, "scalar")
            act.wait_ge(loaded, 16 * N_LOADS)
            act.wait_ge(s["dve_setup"], after(2))
            nc.scalar.activation(bn_tmp[:, 1:2], bn_tmp[:, 0:1], ACT.Sqrt).then_inc(s["act_setup"], 1)
            nc.scalar.activation(A[:, :, :], A[:, :, :], ACT.Exp).then_inc(s["act_setup"], 1)
            act.wait_ge(s["dve_setup"], after(3))

            def take_xt(c, pair):
                act.wait_ge(s["xk_done"], after(c * 2 + pair))
                act.wait_ge(s["s_done"], after(c - 1))
                nc.scalar.activation(x_t[:, 2 * pair:2 * pair + 2, :], xk_ps[:, :, 0:128], ACT.Copy) \
                    .then_inc(s["xt_ready"], 1)

            def key_norms(c):
                act.wait_ge(s["k_red"], after(c))
                nc.scalar.activation(knorm[:, :], knorm[:, :], ACT.Ln).then_inc(s["lnk"], 1)
                act.wait_ge(s["lnk"], after(c))
                nc.scalar.activation(knorm[:, :], knorm[:, :], ACT.Exp, scale=-0.5).then_inc(s["rk_ready"], 1)

            def norm_relu(c):
                act.wait_ge(s["conv_done"], after(c))
                act.wait_ge(s["q_done"], after(c - 1))
                nc.scalar.activation(y_relu[:, :], conv_ps, ACT.Relu, bias=bn_tmp[:, 3:4],
                                     scale=bn_tmp[:, 2:3]).then_inc(s["relu_done"], 1)

            def features(f, par):
                act.wait_ge(s["gt_done"], after(f))
                act.wait_ge(feat_stored[par], (f - par) * 8 + 16)
                act.wait_ge(s["x_done"], after(f * 2 - 1))
                act.wait_ge(s["z_done"], after(f * 2 - 3))
                for k in range(TAPS):
                    shift = TAPS - 1 - k
                    last = nc.scalar.activation(g[32 * k:32 * k + 32, par, shift:shift + CH],
                                                fe[32 * k:32 * k + 32, :], ACT.Copy)
                last.then_inc(s["g_copied"], 1)

            def silu_x(f, par):
                act.wait_ge(s["gated"], after(f - 2))
                for h in range(HALVES):
                    act.wait_ge(s["x_done"], after(f * 2 + h))
                    nc.scalar.activation(xm[:, par, h, :], xz_ps[h], ACT.Silu, bias=conv_b[:, h:h + 1]) \
                        .then_inc(s["x_ready"], 1)

            def silu_z(q, h):
                act.wait_ge(s["gated"], after(q - 1))
                act.wait_ge(s["z_done"], after(q * 2 + h))
                nc.scalar.activation(zs[:, h, :], xz_ps[h], ACT.Silu).then_inc(s["z_ready"], 1)

            def take_dbl(f, par):
                act.wait_ge(s["dbl_done"], after(f))
                act.wait_ge(s["dtm_done"], after(f * 2 - 1))
                act.wait_ge(s["parts_ready"], after(f - 1))
                act.wait_ge(s["b_done"], after(f * S - S - 1))
                act.wait_ge(s["c_done"], after(f * S - S - 1))
                nc.scalar.activation(parts[:, par, :], fe[0:BC3, :], ACT.Copy).then_inc(s["split1"], 1)
                nc.scalar.activation(dbl[:, :], fe[0:BC3 + RANK, :], ACT.Copy).then_inc(s["dbl_ready"], 1)

            def softplus_take(f, h):
                act.wait_ge(s["dt_ready"], after(f - 1))
                act.wait_ge(s["outp_done"], after(f - 2))
                act.wait_ge(s["dtm_done"], after(f * 2 + h))
                nc.scalar.activation(sp_e[:, h, :], fe, ACT.Abs, bias=dt_b[:, h:h + 1]).then_inc(s["sp_abs"], 1)
                nc.scalar.activation(sp_r[:, h, :], fe, ACT.Relu, bias=dt_b[:, h:h + 1]).then_inc(s["sp_lin"], 1)

            def softplus_exp(f):
                act.wait_ge(s["sp_abs"], after(f * 2 + 1))
                nc.scalar.activation(sp_e, sp_e, ACT.Exp, scale=-1.0).then_inc(s["sp_exp"], 1)
                act.wait_ge(s["sp_exp"], after(f))
                act.wait_ge(s["sp4"], after(f - 1))
                nc.scalar.activation(sp_w, sp_e, ACT.Copy, bias=1.0).then_inc(s["sp1"], 1)

            def softplus_log(f):
                act.wait_ge(s["sp2"], after(f))
                nc.scalar.activation(sp_w, sp_w, ACT.Ln).then_inc(s["sp_ln"], 1)

            def decays(q, k):
                if k == 0:
                    act.wait_ge(s["dt_ready"], after(q))
                act.wait_ge(s["scanned"], after(q * UNITS + (k - 2)))
                for h in range(HALVES):
                    for i in range(PAIR):
                        n = PAIR * k + i
                        last = nc.scalar.activation(stretches(decay[k % 2])[:, h, i, 1:SEG], dt[:, h, :], ACT.Exp,
                                                    scale=A[:, h, n:n + 1])
                last.then_inc(s["decay_ready"], 1)

            def take_c(q, k, i):
                if i == 0:
                    act.wait_ge(s["multiplied"], after(q * UNITS + (k - 2)))
                act.wait_ge(s["c_done"], after(q * S + (PAIR * k + i)))
                nc.scalar.activation(c_sb[:, k % 2, i, :], c_ps, ACT.Copy).then_inc(s["c_ready"], 1)

            def take_out(q):
                act.wait_ge(s["outp_done"], after(q))
                act.wait_ge(xr_stored, q * 16 + 16)
                act.wait_ge(s["stat_done"], after(q - 1))
                nc.scalar.activation(xr[:, :], fe, ACT.Copy).then_inc(s["xr_ready"], 1)

            def body(img, w, layer0, first=False, last=False):
                for j in range(BODY):
                    q = img * IMG_CH + w * BODY + j
                    f, c, par = q + 1, q + IMG_CH, j % 2
                    prev, ahead = not (first and j == 0), not (last and j == BODY - 1)
                    for k in range(UNITS):
                        take_c(q, k, 0)
                        if k == 5 and ahead:
                            softplus_take(f, 0)
                        if k < UNITS - 1 and k != 4:
                            decays(q, k + 1)
                        if layer0 and k in (0, 2):
                            take_xt(c, k // 2)
                        if k == 4 and ahead:
                            take_dbl(f, 1 - par)
                        if k == 5 and ahead:
                            softplus_take(f, 1)
                        if k == UNITS - 1 and ahead:
                            softplus_log(f)
                        take_c(q, k, 1)
                        if k == 1 and ahead:
                            features(f, 1 - par)
                        if k == 3:
                            decays(q, 5)
                            if prev:
                                take_out(q - 1)
                            if ahead:
                                silu_x(f, 1 - par)
                            silu_z(q, 0)
                            silu_z(q, 1)
                            act.preload_act_table_set("natural_log_exp_and_others")
                            if layer0:
                                key_norms(c)
                        if k == 5 and ahead:
                            softplus_exp(f)
                        if layer0 and k == 6:
                            norm_relu(c)
                    if ahead:
                        decays(f, 0)

            def section(img, layer0):
                f0 = img * IMG_CH
                features(f0, 0)
                silu_x(f0, 0)
                act.preload_act_table_set("natural_log_exp_and_others")
                take_dbl(f0, 0)
                act.wait_ge(s["outp_done"], after(f0 - 1))
                for h in range(HALVES):
                    softplus_take(f0, h)
                softplus_exp(f0)
                softplus_log(f0)
                decays(f0, 0)
                body(img, 0, layer0, first=True)
                with act.Fori(1, BODIES - 1) as w:
                    body(img, w, layer0)
                body(img, BODIES - 1, layer0, last=True)

            def query_norms(img):
                act.wait_ge(s["q_norm2"], after(img))
                nc.scalar.activation(q_feat[:, :, M:F], q_feat[:, :, M:F], ACT.Sqrt).then_inc(s["qn_ready"], 1)

            act.preload_act_table_set("natural_log_exp_and_others")
            with act.Fori(0, BODIES) as w:
                for j in range(BODY):
                    c = w * BODY + j
                    for pair in range(2):
                        take_xt(c, pair)
                    key_norms(c)
                    norm_relu(c)
            query_norms(0)
            with act.Fori(0, B - 1) as img:
                section(img, True)
                query_norms(img + 1)
                take_out(img * IMG_CH + (IMG_CH - 1))
            section(B - 1, False)
            take_out(CHUNKS - 1)

            act.wait_ge(s["mom1"], after(0))
            nc.scalar.activation(mom[:, 1:2], mom[:, 1:2], ACT.Sqrt).then_inc(s["std_ready"], 1)
            act.wait_ge(s["mom_ready"], after(0))
            with act.Fori(0, B) as img:
                with act.Fori(0, FIN_TURNS) as w:
                    for p in range(FIN_BUFS):
                        it = img * (N // FIN) + w * FIN_BUFS + p
                        act.wait_ge(fin_loaded[p], (img * FIN_TURNS + w) * 32 + 32)
                        nc.scalar.activation(fin_x[p], fin_x[p], ACT.Identity, bias=mom[:, 3:4],
                                             scale=mom[:, 2:3]).then_inc(s["fin_a"], 1)
                        act.wait_ge(s["fin_v"], after(it))
                        act.dma_start(out[bass.ds(img, 1), :, bass.ds((w * FIN_BUFS + p) * FIN, FIN)]
                                      .rearrange("a c n -> (a c) n"), fin_y[p % 2]).then_inc(out_stored[p % 2], 16)

        @block.vector
        def _(dve):
            raise_credit(dve, "vector")
            nc.vector.memset(conv_mask[:, 0:DI], 0.0)
            nc.vector.memset(conv_mask[0:96, DI:2 * DI], 0.0)
            nc.vector.memset(conv_mask[96:128, DI:2 * DI], 1.0).then_inc(s["dve_setup"], 1)
            nc.vector.memset(ones[:, :], 1.0)
            nc.vector.memset(sums[:, :], 0.0)
            nc.vector.memset(kn[:, :, :], 1.0)
            for k in range(2):
                nc.vector.memset(stretches(decay[k])[:, :, :, 0:1], 0.0)
            nc.vector.memset(mv_t4[:, :, :], 0.0)
            nc.vector.memset(g_rep[:, :, :, :], 0.0)
            nc.vector.memset(g[:, :, :], 0.0)
            nc.vector.memset(w_edge[:, :], 0.0)
            nc.vector.memset(carry[:, :, :], 0.0).then_inc(s["dve_setup"], 1)
            dve.wait_ge(loaded, 16 * N_LOADS)
            dve.wait_ge(s["dve_setup"], after(1))
            nc.vector.tensor_scalar(A[:, :, :], A[:, :, :], LOG_MAX, None, ALU.min)
            nc.vector.tensor_scalar(bn_tmp[:, 0:1], bn_v, BN_EPS, None, ALU.add).then_inc(s["dve_setup"], 1)
            dve.wait_ge(s["act_setup"], after(1))
            nc.vector.reciprocal(bn_tmp[:, 1:2], bn_tmp[:, 1:2]).then_inc(s["mom2"], 1)
            dve.wait_ge(s["mom2"], after(0))
            nc.vector.tensor_tensor(bn_tmp[:, 2:3], bn_tmp[:, 1:2], bn_s, ALU.mult).then_inc(s["mom2"], 1)
            dve.wait_ge(s["mom2"], after(1))
            nc.vector.tensor_tensor(bn_tmp[:, 0:1], bn_tmp[:, 2:3], bn_m, ALU.mult).then_inc(s["mom2"], 1)
            dve.wait_ge(s["mom2"], after(2))
            nc.vector.tensor_tensor(bn_tmp[:, 3:4], bn_b, bn_tmp[:, 0:1], ALU.subtract)
            nc.vector.tensor_scalar(A[:, :, :], A[:, :, :], -1.0, None, ALU.mult).then_inc(s["dve_setup"], 1)

            def over_tiles(row, count):
                return row[:, None, :].broadcast_to([128, count, M])

            def take_keys(c, pair):
                dve.wait_ge(s["xt_ready"], after(c * 2 + pair))
                dve.wait_ge(s["kn_ready"], after(c - 1))
                nc.vector.tensor_tensor(keys[:, 2 * pair:2 * pair + 2, :], xk_ps[:, :, 128:],
                                        over_tiles(bk_b, 2), ALU.add).then_inc(s["k_taken"], 1)

            def key_squares(c):
                dve.wait_ge(s["k_taken"], after(c * 2 + 1))
                nc.vector.tensor_tensor(keys_sq[:, :, :], keys[:, :, :], keys[:, :, :], ALU.mult) \
                    .then_inc(s["k_sq"], 1)
                dve.wait_ge(s["k_sq"], after(c))
                nc.vector.tensor_reduce(knorm[:, :], keys_sq[:, :, :], AX.X, ALU.add).then_inc(s["k_red"], 1)

            def normalize_keys(c):
                dve.wait_ge(s["rk_ready"], after(c))
                dve.wait_ge(s["s_done"], after(c - 1))
                nc.vector.tensor_tensor(kn[:, :, 0:M], keys[:, :, :],
                                        knorm[:, :, None].broadcast_to([128, TILES, M]), ALU.mult) \
                    .then_inc(s["kn_ready"], 1)

            def add_sums(c):
                dve.wait_ge(s["s_done"], after(c))
                dve.wait_ge(s["s_taken"], after(c - 1))
                nc.vector.tensor_tensor(sums[:, :], sums[:, :], s_ps, ALU.add).then_inc(s["s_taken"], 1)

            def take_queries(c, local, stored):
                dve.wait_ge(s["q_done"], after(c))
                dve.wait_ge(image_stored, stored)
                nc.vector.tensor_tensor(q_feat[:, bass.ds(local * TILES, TILES), 0:M],
                                        q_ps.rearrange("p (a m) -> p a m", m=M), over_tiles(bq_b, TILES),
                                        ALU.add).then_inc(s["q_taken"], 1)

            def finish_image(img):
                c_last, nt = img * IMG_CH + (IMG_CH - 1), N // 128

                def step(k):
                    dve.wait_ge(s["q_steps"], after(img * 5 + k))

                q, r = q_feat[:, :, 0:M], q_feat[:, :, M]
                dve.wait_ge(s["s_taken"], after(c_last))
                dve.wait_ge(s["q_taken"], after(c_last))
                nc.vector.tensor_scalar(ksum_b[:, :], sums[:, F:F + M], NORM_EPS, None, ALU.add) \
                    .then_inc(s["ksb_ready"], 1)
                nc.vector.tensor_tensor(sq_tmp, q, q, ALU.mult).then_inc(s["q_steps"], 1)
                step(0)
                nc.vector.tensor_reduce(r, sq_tmp, AX.X, ALU.add).then_inc(s["q_norm2"], 1)
                dve.wait_ge(s["mvt_done"], after(img))
                nc.vector.tensor_scalar(mv_t4[:, :, 0:F], mvt_ps[:, None, :].broadcast_to([128, TAPS, F]),
                                        gamma[:, 0:1], None, ALU.mult).then_inc(s["mvt_ready"], 1)
                dve.wait_ge(s["q_norm2"], after(img))
                dve.wait_ge(s["ksb_ready"], after(img))
                nc.vector.tensor_tensor(sq_tmp, q, over_tiles(ksum_b, nt), ALU.mult).then_inc(s["q_steps"], 1)
                step(1)
                nc.vector.tensor_reduce(qk[:, :], sq_tmp, AX.X, ALU.add).then_inc(s["q_steps"], 1)
                dve.wait_ge(s["mv_done"], after(img))
                dve.wait_ge(image_stored, img * 32 + 16)
                nc.vector.tensor_scalar(mv_now[:, :], mv_ps, gamma[0:F, 0:1], None, ALU.mult) \
                    .then_inc(s["mv_ready"], 1)
                dve.wait_ge(s["p4_done"], after(img))
                nc.vector.tensor_tensor(w_xz[:, :], conv_ps, conv_mask[:, :], ALU.mult).then_inc(s["w_ready"], 1)
                dve.wait_ge(s["qn_ready"], after(img))
                step(2)
                nc.vector.scalar_tensor_tensor(qk[:, :], r, float(N), qk[:, :], ALU.mult, ALU.add) \
                    .then_inc(s["q_steps"], 1)
                step(3)
                nc.vector.reciprocal(qk[:, :], qk[:, :]).then_inc(s["q_steps"], 1)
                step(4)
                nc.vector.tensor_tensor(q_feat[:, :, :], q_feat[:, :, :],
                                        qk[:, :, None].broadcast_to([128, nt, F]), ALU.mult).then_inc(s["g_ready"], 1)
                dve.wait_ge(s["mv_done"], after(img))
                nc.vector.memset(sums[:, :], 0.0).then_inc(s["cleared"], 1)
                dve.wait_ge(s["cleared"], after(img))

            def features(f, par):
                dve.wait_ge(tile_loaded[par], (f - par) * 8 + 16)
                dve.wait_ge(s["gt_done"], after(f - 1))
                nc.vector.tensor_copy(g_rep[:, :, :, 0:F],
                                      g_tile[:, par, :, None, :].broadcast_to([128, TILES, TAPS, F])) \
                    .then_inc(s["g_rep_ready"], 1)

            def split(f, par):
                dve.wait_ge(s["split1"], after(f))
                dve.wait_ge(s["dbl_ready"], after(f))
                nc.vector.tensor_tensor(resid[:, :], dbl[0:64, :], parts[0:64, par, :], ALU.subtract) \
                    .then_inc(s["split2"], 1)
                dve.wait_ge(s["split2"], after(f))
                nc.vector.tensor_copy(parts[0:64, par, :], resid[:, :]).then_inc(s["split3"], 1)
                dve.wait_ge(s["split3"], after(f))
                nc.vector.tensor_tensor(resid[0:32, :], resid[0:32, :], parts[0:32, par, :], ALU.subtract) \
                    .then_inc(s["split4"], 1)
                dve.wait_ge(s["split4"], after(f))
                nc.vector.tensor_copy(parts[0:32, par, :], resid[0:32, :]).then_inc(s["parts_ready"], 1)

            def softplus_mid(f):
                dve.wait_ge(s["sp1"], after(f))
                nc.vector.scalar_tensor_tensor(sp_c, sp_w, 1.0, sp_e, ALU.subtract, ALU.subtract).then_inc(s["sp2"], 1)

            def softplus_end(f, par):
                dve.wait_ge(s["sp_ln"], after(f))
                nc.vector.tensor_tensor(sp_c, sp_w, sp_c, ALU.subtract).then_inc(s["sp3"], 1)
                dve.wait_ge(s["sp3"], after(f))
                nc.vector.scalar_tensor_tensor(sp_c, sp_e, 0.5, sp_c, ALU.mult, ALU.max).then_inc(s["sp4"], 1)
                dve.wait_ge(s["sp4"], after(f))
                dve.wait_ge(s["sp_lin"], after(f * 2 + 1))
                dve.wait_ge(s["decay_ready"], after(f * UNITS - 1))
                nc.vector.tensor_tensor(dt[:, :, :], sp_r, sp_c, ALU.add).then_inc(s["dt_ready"], 1)
                dve.wait_ge(s["dt_ready"], after(f))
                dve.wait_ge(s["x_ready"], after(f * 2 + 1))
                nc.vector.tensor_tensor(u[:, par, :, :], dt[:, :, :], xm[:, par, :, :], ALU.mult) \
                    .then_inc(s["u_ready"], 1)

            def fill(q, k, par):
                unit = stretches(state[k % 4])
                dve.wait_ge(s["u_ready"], after(q))
                dve.wait_ge(s["summed"], after(q * UNITS + (k - 4)))
                for i in range(PAIR):
                    dve.wait_ge(s["b_done"], after(q * S + (PAIR * k + i)))
                    nc.vector.tensor_tensor(unit[:, :, i, 1:SEG], u[:, par, :, :],
                                            b_ps[i][:, None, :].broadcast_to([128, HALVES, CH]), ALU.mult) \
                        .then_inc(s["b_used"], 1)
                dve.wait_ge(s["carried"], after(q * UNITS + (k - UNITS)))
                nc.vector.tensor_copy(unit[:, :, :, 0:1], carry[:, k, :].rearrange("c (h n a) -> c h n a", h=HALVES, a=1)) \
                    .then_inc(s["filled"], 1)

            def scan(q, k):
                dve.wait_ge(s["b_used"], after(q * S + (PAIR * k + 1)))
                dve.wait_ge(s["filled"], after(q * UNITS + k))
                dve.wait_ge(s["decay_ready"], after(q * UNITS + k))
                nc.vector.tensor_tensor_scan(state[k % 4], decay[k % 2], state[k % 4], 0.0, ALU.mult, ALU.add) \
                    .then_inc(s["scanned"], 1)
                dve.wait_ge(s["scanned"], after(q * UNITS + k))
                nc.vector.tensor_copy(carry[:, k, :].rearrange("c (h n a) -> c h n a", h=HALVES, a=1),
                                      stretches(state[k % 4])[:, :, :, SEG - 1:SEG]).then_inc(s["carried"], 1)

            def gate(q, par):
                dve.wait_ge(s["summed"], after(q * UNITS + (UNITS - 1)))
                dve.wait_ge(s["outp_done"], after(q - 1))
                dve.wait_ge(s["z_ready"], after(q * 2 + 1))
                for h in range(HALVES):
                    nc.vector.scalar_tensor_tensor(yt[:, h, :], xm[:, par, h, :], Dp[:, h:h + 1], y_ps[h],
                                                   ALU.mult, ALU.add).then_inc(s["y_taken"], 1)
                dve.wait_ge(s["y_taken"], after(q * 2 + 1))
                nc.vector.tensor_tensor(yt, yt, zs[:, :, :], ALU.mult).then_inc(s["gated"], 1)

            def channel_stats(q):
                dve.wait_ge(s["xr_ready"], after(q))
                nc.vector.bn_stats(stats[:, bass.ds(q, 1), :].rearrange("p a k -> p (a k)"), xr[:, :]) \
                    .then_inc(s["stat_done"], 1)

            def body(img, w, layer0, first=False, last=False):
                for j in range(BODY):
                    q = img * IMG_CH + w * BODY + j
                    f, c, par = q + 1, q + IMG_CH, j % 2
                    prev, ahead = not (first and j == 0), not (last and j == BODY - 1)
                    for k in range(UNITS):
                        fill(q, k, par)
                        if k == UNITS - 1 and ahead:
                            softplus_mid(f)
                        scan(q, k)
                        if layer0 and k == 5:
                            normalize_keys(c)
                        if k == 0 and ahead:
                            features(f, 1 - par)
                        if k == 2 and prev:
                            gate(q - 1, 1 - par)
                        if k == 5 and ahead:
                            split(f, 1 - par)
                        if k == 5 and prev:
                            channel_stats(q - 1)
                        if layer0:
                            if k in (1, 2):
                                take_keys(c, k - 1)
                            if k == 3:
                                key_squares(c)
                            if k == 6:
                                add_sums(c)
                    if ahead:
                        softplus_end(f, 1 - par)
                    if layer0:
                        take_queries(c, w * BODY + j, img * 32 + 48)

            def section(img, layer0):
                f0 = img * IMG_CH
                features(f0, 0)
                split(f0, 0)
                softplus_mid(f0)
                softplus_end(f0, 0)
                dve.wait_ge(s["x_done"], after(f0 * 2 + 1))
                nc.vector.tensor_copy(w_edge[:, :], w_xz[:, 0:DI]).then_inc(s["edge_ready"], 1)
                body(img, 0, layer0, first=True)
                with dve.Fori(1, BODIES - 1) as w:
                    body(img, w, layer0)
                body(img, BODIES - 1, layer0, last=True)

            with dve.Fori(0, BODIES) as w:
                for j in range(BODY):
                    c = w * BODY + j
                    for pair in range(2):
                        take_keys(c, pair)
                    key_squares(c)
                    normalize_keys(c)
                    add_sums(c)
                    take_queries(c, c, 16)
            finish_image(0)
            with dve.Fori(0, B - 1) as img:
                section(img, True)
                finish_image(img + 1)
                gate(img * IMG_CH + (IMG_CH - 1), 1)
                channel_stats(img * IMG_CH + (IMG_CH - 1))
            section(B - 1, False)
            gate(CHUNKS - 1, 1)
            channel_stats(CHUNKS - 1)

            dve.wait_ge(s["stat_done"], after(CHUNKS - 1))
            nc.vector.bn_aggr(mom[:, 0:2], stats[:, :, :].rearrange("p a k -> p (a k)")).then_inc(s["mom2"], 1)
            dve.wait_ge(s["mom2"], after(3))
            nc.vector.tensor_scalar(mom[:, 1:2], mom[:, 1:2], BN_EPS, None, ALU.add).then_inc(s["mom1"], 1)
            dve.wait_ge(s["std_ready"], after(0))
            nc.vector.reciprocal(mom[:, 1:2], mom[:, 1:2]).then_inc(s["mom2"], 1)
            dve.wait_ge(s["mom2"], after(4))
            nc.vector.tensor_tensor(mom[:, 2:3], mom[:, 1:2], bn2[:, 0:1], ALU.mult).then_inc(s["mom2"], 1)
            dve.wait_ge(s["mom2"], after(5))
            nc.vector.tensor_tensor(mom[:, 0:1], mom[:, 0:1], mom[:, 2:3], ALU.mult).then_inc(s["mom2"], 1)
            dve.wait_ge(s["mom2"], after(6))
            nc.vector.tensor_tensor(mom[:, 3:4], bn2[:, 1:2], mom[:, 0:1], ALU.subtract).then_inc(s["mom_ready"], 1)
            with dve.Fori(0, B) as img:
                dve.wait_ge(mv_loaded, 16)
                dve.wait_ge(s["fin_mm"], after(img * (N // FIN) - 1))
                nc.vector.tensor_copy(mv_now[:, :], mv_all[:, bass.ds(img, 1), :].rearrange("m a c -> m (a c)")) \
                    .then_inc(s["mvnow_ready"], 1)
                with dve.Fori(0, FIN_TURNS) as w:
                    for p in range(FIN_BUFS):
                        it = img * (N // FIN) + w * FIN_BUFS + p
                        dve.wait_ge(s["fin_a"], after(it))
                        dve.wait_ge(out_stored[p % 2], (img * FIN_TURNS * 2 + w * 2 + p // 2) * 16 + 16)
                        nc.vector.scalar_tensor_tensor(fin_y[p % 2], fin_x[p], 0.2, fin_x[p], ALU.mult, ALU.max) \
                            .then_inc(s["fin_done"], 1)
                        dve.wait_ge(s["fin_done"], after(it))
                        dve.wait_ge(s["fin_mm"], after(it))
                        nc.vector.tensor_tensor(fin_y[p % 2], fin_y[p % 2], fin_ps[p % 2].rearrange("p a n -> p (a n)"),
                                                ALU.add).then_inc(s["fin_v"], 1)

        @block.gpsimd
        def _(pool):
            raise_credit(pool, "gpsimd")

            with pool.Fori(0, CHUNKS) as q:
                for k in range(UNITS):
                    unit = stretches(state[k % 4])
                    pool.wait_ge(s["carried"], after(q * UNITS + k))
                    pool.wait_ge(s["c_ready"], after(q * S + (PAIR * k + PAIR - 1)))
                    nc.gpsimd.tensor_tensor(unit[:, :, :, 1:SEG], unit[:, :, :, 1:SEG],
                                            c_sb[:, k % 2, None, :, :].broadcast_to([128, HALVES, PAIR, CH]),
                                            ALU.mult).then_inc(s["multiplied"], 1)
                    if k in ADDED:
                        pool.wait_ge(s["multiplied"], after(q * UNITS + k))
                        nc.gpsimd.tensor_tensor(unit[:, :, 0, 1:SEG], unit[:, :, 0, 1:SEG], unit[:, :, 1, 1:SEG],
                                                ALU.add).then_inc(s["weighted"], 1)


N_LOADS = 30


def kernel(**inputs):
    import numpy as np
    import ml_dtypes
    import concourse.bacc as bacc
    from concourse import mybir
    from concourse.bass_utils import run_bass_kernel_spmd

    a = {k.replace("L0_conv_", "").replace("L1_conv_", "m_"): np.asarray(v) for k, v in inputs.items()}
    x = np.zeros((B, C, HP, W), np.float32)
    x[:, :, PAD:PAD + H, :] = a["x"]
    taps = [a[f"w{b}"].reshape(32, 128, 9).transpose(1, 2, 0) for b in (2, 3, 4)]
    onehot = np.zeros((3, 2 * S, 2 * S, 128), ml_dtypes.bfloat16)
    for n in range(2 * S):
        onehot[:, n, n, :] = 1
    xp = a["m_x_proj_w"]
    bc = xp[RANK:].T
    halves = lambda v: np.ascontiguousarray(v.reshape(HALVES, 128).T)
    arrays = {
        "x": x, "ident": np.eye(128, dtype=np.float32), "onehot": onehot.reshape(BC3, 2 * S, 128),
        "w_taps": np.concatenate(taps, 1),
        "w_mid": np.concatenate([a["w1"].reshape(32, 128).T] + [p[:, 4] for p in taps], 1),
        "bn_scale": a["bn_scale"].reshape(128, 1), "bn_bias": a["bn_bias"].reshape(128, 1),
        "bn_mean": a["bn_mean"].reshape(128, 1), "bn_var": a["bn_var"].reshape(128, 1),
        "wq": a["wq"].reshape(M, 128).T, "wk": a["wk"].reshape(M, 128).T, "wv": a["wv"].reshape(128, 128).T,
        "bq": a["bq"].reshape(1, M), "bk": a["bk"].reshape(1, M), "bv": a["bv"].reshape(1, 128),
        "gamma": a["gamma"].reshape(1, 1), "w_in": a["m_in_proj_w"].T, "conv_w": a["m_conv_w"].T,
        "conv_b": halves(a["m_conv_b"]),
        "x_proj": np.concatenate([bc, bc, bc, xp[:RANK].T], 1).reshape(HALVES, 128, BC3 + RANK).transpose(1, 0, 2),
        "dt_w": a["m_dt_proj_w"].T, "dt_b": halves(a["m_dt_proj_b"]),
        "A_log": a["m_A_log"].reshape(HALVES, 128, S).transpose(1, 0, 2), "D": halves(a["m_D"]),
        "w_out": a["m_out_proj_w"].T.reshape(HALVES, 128, 128).transpose(1, 0, 2),
        "bn_gamma": a["m_bn_gamma"].reshape(128, 1), "bn_beta": a["m_bn_beta"].reshape(128, 1),
    }
    nc = bacc.Bacc("TRN2", target_bir_lowering=False, num_devices=1)
    feeds, t = {}, {}
    for name, v in arrays.items():
        v = np.ascontiguousarray(v)
        feeds[f"in_{name}"] = v
        t[name] = nc.dram_tensor(f"in_{name}", v.shape, mybir.dt.from_np(v.dtype), kind="ExternalInput").ap()
    out = nc.dram_tensor("out", (B, C, N), mybir.dt.float32, kind="ExternalOutput").ap()
    program(nc, t, out)
    r = run_bass_kernel_spmd(nc, [feeds], core_ids=[0])
    return r.results[0]["out"].reshape(B, C, H, W)
```
